# Optimizing a Trainium2 kernel written in Bass

```python
import numpy as np
import jax
import jax.numpy as jnp

def _softmax(x, axis=-1):
    return jax.nn.softmax(x, axis=axis)

def _gelu(x):
    return jax.nn.gelu(x, approximate=True)

def _silu(x):
    return jax.nn.silu(x)

def _sigmoid(x):
    return jax.nn.sigmoid(x)

def _layernorm(x, axis=-1, eps=1e-05):
    m = jnp.mean(x, axis=axis, keepdims=True)
    v = jnp.var(x, axis=axis, keepdims=True)
    return (x - m) / jnp.sqrt(v + eps)

def _scatter_add(tgt, idx, src, axis=0):
    return tgt.at[idx].add(src)

def _segment_sum(src, seg, n):
    return jax.ops.segment_sum(src, seg, n)
kernel_name = 'mk_adj_ffn_d1_adj_r2_8a59fe'

def setup_inputs(seed: int=0):
    np.random.seed(seed)
    _w = jnp.asarray

    def _rec_inputs():
        import jax
        import jax.numpy as jnp
        _gk = jax.random.key(seed)
        x = 7.22e-05 + 1 * jax.random.normal(jax.random.fold_in(_gk, 1), (8, 2048, 128), jnp.float32)
        _w = (1.0 + jnp.arange(2048, dtype=jnp.float32)) ** (-0.5)
        _w = _w / _w.mean()
        _pij = jnp.clip(0.00390625 * _w[:, None] * _w[None, :], 0.0, 1.0)
        _a = jax.random.uniform(jax.random.fold_in(_gk, 2), (2048, 2048)) < _pij
        _a = jnp.logical_or(_a, jnp.swapaxes(_a, -1, -2))
        _a = jnp.logical_or(_a, jnp.eye(2048, dtype=bool))
        _af = _a.astype(jnp.float32)
        _af = _af * jax.random.uniform(jax.random.fold_in(_gk, 3), (2048, 2048), jnp.float32, 0.05, 0.119748)
        adj = _af
        return (x, adj)
    x, adj = _rec_inputs()

    def _L0_gnn_setup():
        import jax, jax.numpy as jnp
        import numpy as np
        B, N, F_IN, F_OUT = (8, 2048, 128, 128)
        key = jax.random.key(seed)
        k1, k2, k3 = jax.random.split(key, 3)
        H = jax.random.normal(k1, (B, N, F_IN), dtype=jnp.float32)
        W = jax.random.normal(k2, (F_IN, F_OUT), dtype=jnp.float32) * (1.0 / np.sqrt(F_IN))
        A = jax.random.normal(k3, (N, N), dtype=jnp.float32) * (1.414 * np.sqrt(2.0 / (N + N)))
        return {'H': H, 'W': W, 'A': A}
    _L0_gnn_all = _L0_gnn_setup()
    _L0_gnn_in = {k: v for k, v in _L0_gnn_all.items() if k in ('W',)}
    del _L0_gnn_all

    def _L0_ffn_setup():
        import jax, jax.numpy as jnp
        import numpy as np
        NUM_EXPERTS = 8
        TOP_K = 2
        B, S, D = (8, 4096, 128)

        def _moe(tokens, router_w, w1, b1, w2, b2):
            N = tokens.shape[0]
            E = router_w.shape[0]
            logits = tokens.astype(jnp.float32) @ router_w.astype(jnp.float32).T
            probs = jax.nn.softmax(logits, axis=-1)
            rw, re = jax.lax.top_k(probs, TOP_K)
            if TOP_K > 1:
                rw = rw / jnp.maximum(rw.sum(-1, keepdims=True), 1e-12)
            rw = rw.astype(tokens.dtype)
            combine = jnp.zeros((N, E), tokens.dtype).at[jnp.arange(N)[:, None], re].set(rw)
            out = tokens
            for e in range(E):
                h = jax.nn.gelu(tokens @ w1[e] + b1[e], approximate=False)
                y = h @ w2[e] + b2[e]
                out = out + combine[:, e:e + 1] * y
            return out
        key = jax.random.key(seed)
        ks = jax.random.split(key, 4)
        scale = 1.0 / np.sqrt(D).astype(np.float32)
        return {'input_embeddings': jax.random.normal(ks[0], (B, S, D), jnp.float32), 'router_w': jax.random.normal(ks[1], (NUM_EXPERTS, D), jnp.float32) * scale, 'w1': jax.random.normal(ks[2], (NUM_EXPERTS, D, D), jnp.float32) * scale, 'b1': jnp.zeros((NUM_EXPERTS, D), jnp.float32), 'w2': jax.random.normal(ks[3], (NUM_EXPERTS, D, D), jnp.float32) * scale, 'b2': jnp.zeros((NUM_EXPERTS, D), jnp.float32)}
    _L0_ffn_all = _L0_ffn_setup()
    _L0_ffn_in = {k: v for k, v in _L0_ffn_all.items() if k in ('router_w', 'w1', 'b1', 'w2', 'b2')}
    del _L0_ffn_all
    return {'x': x, 'adj': adj, 'L0_gnn_W': _L0_gnn_in['W'], 'L0_ffn_router_w': _L0_ffn_in['router_w'], 'L0_ffn_w1': _L0_ffn_in['w1'], 'L0_ffn_b1': _L0_ffn_in['b1'], 'L0_ffn_w2': _L0_ffn_in['w2'], 'L0_ffn_b2': _L0_ffn_in['b2']}

def reference(x, adj, L0_gnn_W, L0_ffn_router_w, L0_ffn_w1, L0_ffn_b1, L0_ffn_w2, L0_ffn_b2):
    import jax
    import jax.numpy as jnp

    def _L0_gnn_ref(H, W, A):
        import jax, jax.numpy as jnp
        import numpy as np
        B, N, F_IN, F_OUT = (8, 2048, 128, 128)
        HW = jnp.einsum('bnf,fo->bno', H, W)
        A_norm = jax.nn.relu((A + A.T) * 0.5)
        D = jnp.sum(A_norm, axis=1)
        D_safe = jnp.where(D > 0, D, 1.0)
        d_inv_sqrt = jnp.where(D > 0, D_safe ** (-0.5), 0.0)
        DAD = d_inv_sqrt[:, None] * A_norm * d_inv_sqrt[None, :]
        L_norm = jnp.eye(N, dtype=H.dtype) - DAD
        out = jnp.einsum('nm,bmo->bno', L_norm, HW)
        return jax.nn.relu(out)

    def _L0_ffn_ref(input_embeddings, router_w, w1, b1, w2, b2):
        import jax, jax.numpy as jnp
        import numpy as np
        NUM_EXPERTS = 8
        TOP_K = 2
        B, S, D = (8, 4096, 128)

        def _moe(tokens, router_w, w1, b1, w2, b2):
            N = tokens.shape[0]
            E = router_w.shape[0]
            logits = tokens.astype(jnp.float32) @ router_w.astype(jnp.float32).T
            probs = jax.nn.softmax(logits, axis=-1)
            rw, re = jax.lax.top_k(probs, TOP_K)
            if TOP_K > 1:
                rw = rw / jnp.maximum(rw.sum(-1, keepdims=True), 1e-12)
            rw = rw.astype(tokens.dtype)
            combine = jnp.zeros((N, E), tokens.dtype).at[jnp.arange(N)[:, None], re].set(rw)
            out = tokens
            for e in range(E):
                h = jax.nn.gelu(tokens @ w1[e] + b1[e], approximate=False)
                y = h @ w2[e] + b2[e]
                out = out + combine[:, e:e + 1] * y
            return out
        b, s, d = input_embeddings.shape
        tokens = input_embeddings.reshape(b * s, d)
        return _moe(tokens, router_w, w1, b1, w2, b2).reshape(b, s, d)
    x = x + _L0_gnn_ref(_layernorm(x, axis=-1), L0_gnn_W, adj)
    x = x + _L0_ffn_ref(_layernorm(x, axis=-1), L0_ffn_router_w, L0_ffn_w1, L0_ffn_b1, L0_ffn_w2, L0_ffn_b2)
    return x

_drawn_inputs = setup_inputs


def setup_inputs(seed=0):
    import zlib

    import numpy as np

    out = dict(_drawn_inputs(seed))
    spreads = {'L0_ffn_b1': (0.0, 0.354), 'L0_ffn_b2': (0.0, 0.1)}
    factors = {}
    for name, (base, spread) in spreads.items():
        noise = np.random.default_rng([zlib.crc32(name.encode()), seed]).standard_normal(out[name].shape)
        drawn = base * np.exp(spread * noise) if base else spread * noise
        out[name] = jnp.asarray(drawn.astype(out[name].dtype))
    for name, factor in factors.items():
        out[name] = (out[name] * factor).astype(out[name].dtype)
    return out
```

```python
import concourse.bass as bass
from concourse import mybir
from contextlib import ExitStack

FP32 = mybir.dt.float32
FP32R = mybir.dt.float32r
U32 = mybir.dt.uint32
ALU = mybir.AluOpType
ACT = mybir.ActivationFunctionType
AX = mybir.AxisListType

P = 128


class Plan:
    pass


def gnn_moe_kernel(nc, x, adj, gnn_w, router_w, w1, b1, w2, b2, out):
    B, N, D = x.shape
    E = router_w.shape[0]
    MB = N // P
    CW = 512
    NC = N // CW
    Q = CW // P
    U = NC * B
    PAIRS = B // 2
    v = Plan()
    v.x, v.adj, v.gnn_w, v.router_w, v.w1, v.b1, v.w2, v.b2, v.out = x, adj, gnn_w, router_w, w1, b1, w2, b2, out
    v.B, v.N, v.D, v.E, v.MB, v.CW, v.NC, v.Q, v.U, v.PAIRS = B, N, D, E, MB, CW, NC, Q, U, PAIRS
    v.EPS = 1e-5
    assert D == P and N % CW == 0 and B % 2 == 0 and E == 8 and PAIRS == NC

    v.s_dram = nc.dram_tensor("s_scratch", (NC, P, MB, CW), FP32, kind="Internal").ap()
    v.xn_dram = nc.dram_tensor("xn_scratch", (B, P, MB, D), FP32, kind="Internal").ap()
    v.z_dram = nc.dram_tensor("z_scratch", (U, P, 2, CW), FP32, kind="Internal").ap()
    v.c_dram = nc.dram_tensor("c_scratch", (U, 2 * E, CW), FP32, kind="Internal").ap()
    v.res_dram = nc.dram_tensor("res_scratch", (U, P, CW), FP32, kind="Internal").ap()

    ctx = ExitStack()
    with ctx:
        limit = nc.sbuf_usable_end
        cursor = [nc.sbuf_base]

        def sb(name, shape, dt, at=None):
            c = cursor if at is None else at
            size = 4
            for n in shape[1:]:
                size *= n
            c[0] = (c[0] + 63) // 64 * 64
            t = nc.alloc_sbuf_tensor_at(name, shape, dt, offset=c[0])
            c[0] += size
            return t

        def sem(name):
            return ctx.enter_context(nc.semaphore(name))

        v.banks = [ctx.enter_context(nc.psum_tensor(f"bank{i}", [P, 512], FP32)) for i in range(8)]

        v.ident = sb("ident", [P, P], FP32)
        v.ones = sb("ones", [P, P], FP32)
        v.neg_half = sb("neg_half", [P, MB], FP32)
        v.iota_e = sb("iota_e", [P, Q, E], FP32)
        v.gnn_w_sb = sb("gnn_w_sb", [P, P], FP32)
        v.rwt_sb = sb("rwt_sb", [P, E], FP32)
        v.b1_sb = sb("b1_sb", [P, E], FP32)
        v.d_row = sb("d_row", [P, N], FP32)
        v.d_col = sb("d_col", [P, 2 * MB], FP32)
        base = cursor[0]

        at = [base]
        v.low = [sb(f"low{i}", [P, N], FP32, at) for i in range(3)]
        v.up = [sb(f"up{i}", [P, MB - 1, P], FP32, at) for i in range(3)]
        v.total = [sb(f"total{i}", [P, CW], FP32, at) for i in range(4)]
        v.s_low = [sb(f"s_low{i}", [P, N], FP32, at) for i in range(2)]
        v.s_up = [sb(f"s_up{i}", [P, MB - 1, P], FP32, at) for i in range(2)]
        v.deg_low = sb("deg_low", [P, MB, NC], FP32, at)
        v.deg_up = sb("deg_up", [P, MB, MB], FP32, at)
        v.deg_parts = sb("deg_parts", [P, 2, MB], FP32, at)
        v.deg = sb("deg", [P, MB], FP32, at)
        v.deg_pos = sb("deg_pos", [P, MB], FP32, at)
        v.deg_safe = sb("deg_safe", [P, MB], FP32, at)
        v.deg_root = sb("deg_root", [P, MB], FP32, at)
        v.d_inv = sb("d_inv", [P, MB], FP32, at)
        v.diag_d = sb("diag_d", [P, Q, P], FP32, at)
        v.x_in = [sb(f"x_in{i}", [P, MB, P], FP32, at) for i in range(2)]
        v.xn_out = [sb(f"xn_out{i}", [P, MB, P], FP32, at) for i in range(2)]
        v.stats0 = sb("stats0", [P, MB, 6], FP32, at)
        v.mv0 = [sb(f"mv0{i}", [P, MB, 2], FP32, at) for i in range(2)]
        v.var_eps0 = sb("var_eps0", [P, MB], FP32, at)
        v.rstd0 = sb("rstd0", [P, MB], FP32, at)
        assert at[0] <= limit, at

        at = [base]
        v.l_hi = [sb(f"l_hi{i}", [P, MB, CW], FP32R, at) for i in range(2)]
        v.l_lo = [sb(f"l_lo{i}", [P, MB, CW], FP32R, at) for i in range(2)]
        v.s_st = sb("s_st", [P, Q, CW], FP32, at)
        v.xn_in = [sb(f"xn_in{i}", [P, MB // 2, P], FP32, at) for i in range(2)]
        v.x_hi = [sb(f"x_hi{i}", [P, MB // 2, P], FP32R, at) for i in range(2)]
        v.x_lo = [sb(f"x_lo{i}", [P, MB // 2, P], FP32R, at) for i in range(2)]
        v.x_res = sb("x_res", [P, Q, P], FP32, at)
        v.y_t = sb("y_t", [P, CW], FP32, at)
        v.x1 = sb("x1", [P, Q, P], FP32, at)
        v.z = sb("z", [P, Q, P], FP32, at)
        v.res = sb("res", [P, Q, P], FP32, at)
        v.z_t = sb("z_t", [P, CW], FP32, at)
        v.z_hl = sb("z_hl", [P, 2, CW], FP32R, at)
        v.stats = sb("stats", [P, Q, 6], FP32, at)
        v.mv = sb("mv", [P, Q, 2], FP32, at)
        v.var_eps = sb("var_eps", [P, Q], FP32, at)
        v.rstd = sb("rstd", [P, Q], FP32, at)
        v.logits = sb("logits", [P, Q, E], FP32, at)
        v.top_val = sb("top_val", [P, Q, 8], FP32, at)
        v.top_idx = sb("top_idx", [P, Q, 8], U32, at)
        v.top_idx_f = sb("top_idx_f", [P, Q, 2], FP32, at)
        v.shifted = sb("shifted", [P, Q, E], FP32, at)
        v.expo = sb("expo", [P, Q, E], FP32, at)
        v.is_1st = sb("is_1st", [P, Q, E], FP32, at)
        v.is_2nd = sb("is_2nd", [P, Q, E], FP32, at)
        v.is_top = sb("is_top", [P, Q, E], FP32, at)
        v.picked = sb("picked", [P, Q, E], FP32, at)
        v.sum_all = sb("sum_all", [P, Q], FP32, at)
        v.sum_top = sb("sum_top", [P, Q], FP32, at)
        v.guarded = sb("guarded", [P, Q], FP32, at)
        v.inv_top = sb("inv_top", [P, Q], FP32, at)
        v.gate = sb("gate", [P, Q, E], FP32, at)
        v.gate_hl = sb("gate_hl", [P, Q, 2 * E], FP32, at)
        v.gate_t = sb("gate_t", [2 * E, CW], FP32, at)
        assert at[0] <= limit, at

        at = [base]
        v.w_raw = sb("w_raw", [P, 2, E, P], FP32, at)
        v.b2_raw = sb("b2_raw", [P, P], FP32, at)
        v.pick_raw = sb("pick_raw", [P, E, P], FP32, at)
        v.w1_hi = sb("w1_hi", [P, E, P], FP32R, at)
        v.w1_lo = sb("w1_lo", [P, E, P], FP32R, at)
        v.w2_hi = sb("w2_hi", [P, E, P], FP32R, at)
        v.w2_lo = sb("w2_lo", [P, E, P], FP32R, at)
        v.b2_hi = sb("b2_hi", [P, P], FP32R, at)
        v.b2_lo = sb("b2_lo", [P, P], FP32R, at)
        v.pick = sb("pick", [P, E, P], FP32R, at)
        v.z_e = [sb(f"z_e{i}", [P, 2, CW], FP32R, at) for i in range(2)]
        v.c_e = [sb(f"c_e{i}", [P, CW], FP32R, at) for i in range(2)]
        v.c_zero = sb("c_zero", [P, CW], FP32, at)
        v.r_e = [sb(f"r_e{i}", [P, CW], FP32, at) for i in range(2)]
        R = v.R = 4
        v.act_h = [sb(f"act_h{i}", [P, CW], FP32, at) for i in range(R)]
        v.gated = [sb(f"gated{i}", [P, CW], FP32, at) for i in range(R)]
        v.g_hi = [sb(f"g_hi{i}", [P, CW], FP32R, at) for i in range(R)]
        v.g_lo = [sb(f"g_lo{i}", [P, CW], FP32R, at) for i in range(R)]
        v.o_t = sb("o_t", [P, CW], FP32, at)
        v.fin = [sb(f"fin{i}", [P, CW], FP32, at) for i in range(2)]
        assert at[0] <= limit, at

        build_setup(nc, sem, v)
        build_graph(nc, sem, v)
        build_experts(nc, sem, v)


def build_setup(nc, sem, v):
    B, N, D, E, MB, CW, NC, Q = v.B, v.N, v.D, v.E, v.MB, v.CW, v.NC, v.Q
    low, up, total, s_low, s_up = v.low, v.up, v.total, v.s_low, v.s_up
    ident, ones = v.ident, v.ones

    low_in = [sem(f"low_in{i}") for i in range(3)]
    up_in = [sem(f"up_in{i}") for i in range(3)]
    consts_made = sem("consts_made")
    turned = sem("turned")
    summed = sem("summed")
    relued = sem("relued")
    deg_added = sem("deg_added")
    low_out = [sem(f"low_out{i}") for i in range(2)]
    up_out = [sem(f"up_out{i}") for i in range(2)]
    deg_ready = sem("deg_ready")
    root_ready = sem("root_ready")
    diag_ready = sem("diag_ready")
    d_spread = sem("d_spread")
    d_row_ready = sem("d_row_ready")
    x_in_ready = [sem(f"x_in_ready{i}") for i in range(2)]
    ln_mv = sem("ln_mv")
    ln_var = sem("ln_var")
    ln_rstd = sem("ln_rstd")
    xn_made = sem("xn_made")
    xn_stored = [sem(f"xn_stored{i}") for i in range(2)]
    small_in = sem("small_in")
    safe_step = sem("safe_step")

    def groups(k):
        out = [("low", k, g, Q * g, min(Q, k + 1 - Q * g)) for g in range(k // Q + 1)]
        out += [("up", k, g, Q * g, min(Q, k - Q * g)) for g in range((k + Q - 1) // Q)]
        return out

    every = [g for k in range(MB) for g in groups(k)]
    number = {g[:3]: n for n, g in enumerate(every)}
    last_of_step = [max(number[g[:3]] for g in groups(k)) + 1 for k in range(MB)]
    LNB = 4

    with nc.Block() as block:

        @block.sync
        def _(sp):
            for k in range(MB):
                s = k % 3
                if k >= 3:
                    sp.wait_ge(summed, last_of_step[k - 3])
                sp.dma_start(low[s][:, 0:(k + 1) * P], v.adj[k * P:(k + 1) * P, 0:(k + 1) * P]).then_inc(low_in[s], 16)
                if k:
                    sp.dma_start(up[s][:, 0:k, :],
                                 v.adj[0:k * P, k * P:(k + 1) * P].rearrange("(j p) n -> p j n", p=P)).then_inc(up_in[s], 16)
            with sp.Fori(0, B // 2) as h:
                for s in range(2):
                    for i in range(2):
                        rows = v.x[bass.ds(2 * h + s, 1)][:, i * N // 2:(i + 1) * N // 2, :]
                        sp.dma_start(v.x_in[s][:, i * MB // 2:(i + 1) * MB // 2, :],
                                     rows.rearrange("a (m p) f -> p (a m) f", p=P)).then_inc(x_in_ready[s], 16)
                for s in range(2):
                    sp.wait_ge(xn_made, 2 * h + s + 1)
                    sp.dma_start(v.xn_dram[bass.ds(2 * h + s, 1)].rearrange("a p m f -> p (a m) f"),
                                 v.xn_out[s][:, :, :]).then_inc(xn_stored[s], 16)
            for s in range(2):
                sp.wait_ge(xn_stored[s], 16 * (B // 2))

        @block.gpsimd
        def _(pool):
            pool.memset(ident[:, :], 0.0).then_inc(consts_made, 1)
            pool.memset(ones[:, :], 1.0).then_inc(consts_made, 1)
            pool.memset(v.neg_half[:, :], -0.5).then_inc(consts_made, 1)
            for e in range(E):
                pool.memset(v.iota_e[:, :, e:e + 1], float(e)).then_inc(consts_made, 1)
            pool.wait_ge(consts_made, 3 + E)
            pool.affine_select(out=ident[:, :], in_=ident[:, :], compare_op=ALU.not_equal, fill=1.0,
                               base=0, pattern=[[-1, P]], channel_multiplier=1).then_inc(consts_made, 1)
            pool.wait_ge(deg_ready, 6)
            pool.tensor_tensor(out=v.deg_root[:, :], in0=v.deg_safe[:, :], in1=v.neg_half[:, :],
                               op=ALU.pow).then_inc(root_ready, 1)
            with pool.Fori(0, B) as b:
                pool.wait_ge(ln_var, b + 1)
                pool.tensor_tensor(out=v.rstd0[:, :], in0=v.var_eps0[:, :], in1=v.neg_half[:, :],
                                   op=ALU.pow).then_inc(ln_rstd, 1)

        @block.scalar
        def _(act):
            act.dma_start(v.gnn_w_sb[:, :], v.gnn_w).then_inc(small_in, 16)
            with nc.allow_non_contiguous_dma(reason="small transposed constants"):
                act.dma_start(v.rwt_sb[:, :], v.router_w.rearrange("e d -> d e")).then_inc(small_in, 16)
                act.dma_start(v.b1_sb[:, :], v.b1.rearrange("e h -> h e")).then_inc(small_in, 16)
            for n, (kind, k, g, j0, nj) in enumerate(every):
                act.wait_ge(summed, n + 1)
                if (kind, g) == ("low", 0) and k >= 2:
                    act.wait_ge(low_out[k % 2], 16 * sum(1 + (kk % Q != Q - 1 and kk >= Q) for kk in range(k % 2, k, 2)))
                if (kind, g) == ("up", 0) and k >= 3:
                    act.wait_ge(up_out[k % 2], 16 * len([kk for kk in range(1, k) if kk % 2 == k % 2]))
                    act.wait_ge(deg_added, k - 2)
                src = v.total[n % 4][:, 0:nj * P]
                if kind == "low":
                    act.activation(s_low[k % 2][:, j0 * P:(j0 + nj) * P], src, ACT.Relu,
                                   accum_out=v.deg_low[:, k, g:g + 1]).then_inc(relued, 1)
                else:
                    act.activation(s_up[k % 2][:, j0:j0 + nj, :].rearrange("p a f -> p (a f)"), src,
                                   ACT.Relu).then_inc(relued, 1)
                if n + 1 == last_of_step[k]:
                    act.wait_ge(relued, n + 1)
                    full = (k + 1) // Q
                    if full:
                        act.dma_start(v.s_dram[0:full, :, k, :].rearrange("c p n -> p c n"),
                                      s_low[k % 2][:, 0:full * CW].rearrange("p (c n) -> p c n", c=full)).then_inc(low_out[k % 2], 16)
                    if full * Q < k + 1:
                        act.dma_start(v.s_dram[full, :, k, 0:(k + 1) * P - full * CW],
                                      s_low[k % 2][:, full * CW:(k + 1) * P]).then_inc(low_out[k % 2], 16)
                    if k:
                        act.dma_start(v.s_dram[k // Q, :, 0:k, (k % Q) * P:(k % Q + 1) * P],
                                      s_up[k % 2][:, 0:k, :]).then_inc(up_out[k % 2], 16)
            act.wait_ge(small_in, 48)
            for c in range(NC):
                act.wait_ge(d_spread, c + 1)
                act.activation(v.d_row[:, c * CW:(c + 1) * CW], v.banks[4 + c % 2][:, :], ACT.Copy).then_inc(d_row_ready, 1)
            for s in range(2):
                act.wait_ge(low_out[s], 16 * sum(1 + (kk % Q != Q - 1 and kk >= Q) for kk in range(s, MB, 2)))
                act.wait_ge(up_out[s], 16 * len([kk for kk in range(1, MB) if kk % 2 == s]))

        @block.tensor
        def _(pe):
            pe.wait_ge(consts_made, 4 + E)
            for n, (kind, k, g, j0, nj) in enumerate(every):
                s = k % 3
                if (kind, g) == ("low", 0):
                    pe.wait_ge(low_in[s], 16 * (k // 3 + 1))
                    if k:
                        pe.wait_ge(up_in[s], 16 * len([kk for kk in range(1, k + 1) if kk % 3 == s]))
                if n >= LNB:
                    pe.wait_ge(summed, n - LNB + 1)
                bank = v.banks[n % LNB]
                for i in range(nj):
                    j = j0 + i
                    src = up[s][:, j, :] if kind == "low" and j < k else low[s][:, j * P:(j + 1) * P]
                    last = pe.transpose(bank[:, i * P:(i + 1) * P], src, ident[:, :])
                last.then_inc(turned, 1)
            for c in range(NC):
                pe.wait_ge(diag_ready, c + 1)
                if c >= 2:
                    pe.wait_ge(d_row_ready, c - 1)
                pe.matmul(v.banks[4 + c % 2][:, :], ones[:, :],
                          v.diag_d[:, :, :].rearrange("p a f -> p (a f)"), start=True, stop=True).then_inc(d_spread, 1)

        @block.vector
        def _(dve):
            dve.memset(v.deg_low[:, :, :], 0.0).then_inc(deg_ready, 1)
            dve.memset(v.deg_up[:, :, :], 0.0).then_inc(deg_ready, 1)
            dve.wait_ge(deg_ready, 2)
            for n, (kind, k, g, j0, nj) in enumerate(every):
                s = k % 3
                dve.wait_ge(turned, n + 1)
                if n >= 4:
                    dve.wait_ge(relued, n - 3)
                src = (low[s][:, j0 * P:(j0 + nj) * P] if kind == "low"
                       else up[s][:, j0:j0 + nj, :].rearrange("p a f -> p (a f)"))
                dve.tensor_tensor(out=v.total[n % 4][:, 0:nj * P], in0=v.banks[n % LNB][:, 0:nj * P], in1=src,
                                  op=ALU.add).then_inc(summed, 1)
                if kind == "up" and j0 + nj == k:
                    dve.wait_ge(relued, n + 1)
                    dve.tensor_reduce(out=v.deg_up[:, k, 0:k], in_=s_up[k % 2][:, 0:k, :], axis=AX.X,
                                      op=ALU.add).then_inc(deg_added, 1)
            dve.wait_ge(relued, len(every))
            dve.wait_ge(deg_added, MB - 1)
            dve.tensor_reduce(out=v.deg_parts[:, 0, :], in_=v.deg_low[:, :, :], axis=AX.X, op=ALU.add)
            dve.tensor_reduce(out=v.deg_parts[:, 1, :], in_=v.deg_up[:, :, :].rearrange("p k j -> p j k"),
                              axis=AX.X, op=ALU.add).then_inc(deg_ready, 1)
            dve.wait_ge(deg_ready, 3)
            dve.tensor_tensor(out=v.deg[:, :], in0=v.deg_parts[:, 0, :], in1=v.deg_parts[:, 1, :], op=ALU.add).then_inc(deg_ready, 1)
            dve.wait_ge(deg_ready, 4)
            dve.tensor_scalar(v.deg_pos[:, :], v.deg[:, :], 0.0, None, ALU.is_gt).then_inc(deg_ready, 1)
            dve.wait_ge(deg_ready, 5)
            dve.tensor_scalar(v.deg_parts[:, 0, :], v.deg_pos[:, :], -1.0, 1.0, ALU.mult, ALU.add).then_inc(safe_step, 1)
            dve.wait_ge(safe_step, 1)
            dve.scalar_tensor_tensor(out=v.deg_safe[:, :], in0=v.deg[:, :], scalar=0.5, in1=v.deg_parts[:, 0, :],
                                     op0=ALU.mult, op1=ALU.add).then_inc(deg_ready, 1)
            dve.wait_ge(root_ready, 1)
            dve.tensor_tensor(out=v.d_inv[:, :], in0=v.deg_root[:, :], in1=v.deg_pos[:, :], op=ALU.mult).then_inc(deg_ready, 1)
            dve.wait_ge(deg_ready, 7)
            for half in range(2):
                dve.tensor_scalar(v.d_col[:, half * MB:(half + 1) * MB], v.d_inv[:, :], -0.5, None, ALU.mult).then_inc(deg_ready, 1)
            for c in range(NC):
                if c:
                    dve.wait_ge(d_spread, c)
                dve.tensor_tensor(out=v.diag_d[:, :, :], in0=ident[:, None, :].to_broadcast([P, Q, P]),
                                  in1=v.d_inv[:, c * Q:(c + 1) * Q][:, :, None].to_broadcast([P, Q, P]),
                                  op=ALU.mult).then_inc(diag_ready, 1)
            def normalise(h, s):
                b = 2 * h + s
                dve.wait_ge(x_in_ready[s], 32 * (h + 1))
                for m in range(MB):
                    last = dve.bn_stats(out=v.stats0[:, m, :], in_=v.x_in[s][:, m, :])
                dve.drain()
                for m in range(MB):
                    last = dve.bn_aggr(out=v.mv0[0][:, m, :], in_=v.stats0[:, m, :])
                last.then_inc(ln_mv, 1)
                dve.wait_ge(ln_mv, b + 1)
                dve.tensor_scalar(v.var_eps0[:, :], v.mv0[0][:, :, 1], v.EPS, None, ALU.add).then_inc(ln_var, 1)
                dve.wait_ge(ln_rstd, b + 1)
                for m in range(MB):
                    last = dve.tensor_scalar(v.xn_out[s][:, m, :], v.x_in[s][:, m, :], v.mv0[0][:, m, 0:1],
                                             v.rstd0[:, m:m + 1], ALU.subtract, ALU.mult)
                last.then_inc(xn_made, 1)

            for s in range(2):
                normalise(0, s)
            with dve.Fori(1, B // 2) as h:
                for s in range(2):
                    dve.wait_ge(xn_stored[s], 16 * h)
                    normalise(h, s)


def wait(eng, semaphore, n):
    if not isinstance(n, int) or n > 0:
        eng.wait_ge(semaphore, n)


def build_graph(nc, sem, v):
    B, E, MB, CW, NC, Q, U, PAIRS = v.B, v.E, v.MB, v.CW, v.NC, v.Q, v.U, v.PAIRS
    ident = v.ident
    HB = MB // 2
    acc = [v.banks[0], v.banks[1]]
    ps_w, ps_z, ps_r, ps_c = v.banks[2], v.banks[3], v.banks[4], v.banks[5]

    xn_loaded = [sem(f"xn_loaded{i}") for i in range(2)]
    x_hi_done = sem("x_hi_done")
    x_lo_done = sem("x_lo_done")
    half_used = sem("half_used")
    s_loaded = sem("s_loaded")
    l_scaled = sem("l_scaled")
    l_made = sem("l_made")
    l_hi_done = sem("l_hi_done")
    l_lo_done = sem("l_lo_done")
    acc_copied = sem("acc_copied")
    w_done = sem("w_done")
    x_res_in = sem("x_res_in")
    x1_done = sem("x1_done")
    mv_done = sem("mv_done")
    var_done = sem("var_done")
    rstd_done = sem("rstd_done")
    z_done = sem("z_done")
    res_done = sem("res_done")
    zt_done = sem("zt_done")
    z_t_done = sem("z_t_done")
    z_hi_done = sem("z_hi_done")
    z_lo_done = sem("z_lo_done")
    logits_done = sem("logits_done")
    logits_copied = sem("logits_copied")
    idx_done = sem("idx_done")
    shift_done = sem("shift_done")
    exp_done = sem("exp_done")
    route_step = sem("route_step")
    gate_done = sem("gate_done")
    gate_turned = sem("gate_turned")
    gate_copied = sem("gate_copied")
    res_stored = sem("res_stored")
    z_stored = sem("z_stored")
    gate_stored = sem("gate_stored")
    gate_step = sem("gate_step")
    ROUTE_STEPS = 8


    def over_units(eng, body):
        for c in range(NC):
            for s in range(2):
                body(c, 0, s, B * c + s, False)
            end = PAIRS - (c == NC - 1)
            with eng.Fori(1, end) as p:
                for s in range(2):
                    body(c, p, s, 2 * p + (B * c + s), False)
        for s in range(2):
            body(NC - 1, PAIRS - 1, s, U - 2 + s, s == 1)

    with nc.Block() as block:

        @block.sync
        def _(sp):
            def load_s(c, r):
                first = (r + c) % NC * Q
                wait(sp, l_lo_done, NC * c + r)
                sp.dma_start(v.s_st[:, :, :], v.s_dram[c][:, first:first + Q, :]).then_inc(s_loaded, 16)

            def load_x(c, b, u, half):
                wait(sp, x_lo_done, 2 * u + half - 1)
                for i in range(2):
                    g = (c + 2 * half + i) % NC
                    sp.dma_start(v.xn_in[half][:, i * Q:(i + 1) * Q, :],
                                 v.xn_dram[b, :, g * Q:(g + 1) * Q, :]
                                 ).then_inc(xn_loaded[half], 16)

            load_s(0, 0)
            load_x(0, 0, 0, 0)
            load_s(0, 1)
            load_s(0, 2)
            load_x(0, 0, 0, 1)
            load_s(0, 3)

            for c, b in ((c, b) for c in range(NC) for b in range(B)):
                u = B * c + b
                if u:
                    load_x(c, b, u, 0)
                    load_x(c, b, u, 1)
                wait(sp, x1_done, u)
                sp.dma_start(v.x_res[:, :, :],
                             v.x[b, c * CW:(c + 1) * CW, :].rearrange("(q p) f -> p q f", p=P)
                             ).then_inc(x_res_in, 16)
                if b % 2 == 0 and c + 1 < NC:
                    load_s(c + 1, b // 2)


        @block.tensor
        def _(pe):
            def propagate(c, s, u, half, blocks):
                for i in blocks:
                    r = half * HB + i
                    xh, xl = v.x_hi[half][:, i, :], v.x_lo[half][:, i, :]
                    lh, ll = v.l_hi[c % 2][:, r, :], v.l_lo[c % 2][:, r, :]
                    pe.matmul(acc[s][:, :], xh, lh, start=(r == 0), stop=False)
                    pe.matmul(acc[s][:, :], xh, ll, start=False, stop=False)
                    last = pe.matmul(acc[s][:, :], xl, lh, start=False, stop=(r == MB - 1))
                if blocks[-1] == HB - 1:
                    last.then_inc(half_used, 1)

            def project(u):
                pe.wait_ge(acc_copied, u + 1)
                wait(pe, x1_done, u)
                for q in range(Q):
                    last = pe.matmul(ps_w[:, q * P:(q + 1) * P], v.y_t[:, q * P:(q + 1) * P], v.gnn_w_sb[:, :],
                                     start=True, stop=True)
                last.then_inc(w_done, 1)

            def turn_z(u):
                pe.wait_ge(z_done, u + 1)
                for q in range(Q):
                    last = pe.transpose(ps_z[:, q * P:(q + 1) * P], v.z[:, q, :], ident[:, :])
                last.then_inc(zt_done, 1)

            def route(u):
                pe.wait_ge(z_t_done, u + 1)
                wait(pe, logits_copied, u)
                for q in range(Q):
                    last = pe.matmul(ps_r[:, q * E:(q + 1) * E], v.z_t[:, q * P:(q + 1) * P], v.rwt_sb[:, :],
                                     start=True, stop=True)
                last.then_inc(logits_done, 1)

            def turn_gate(u):
                pe.wait_ge(gate_done, u + 1)
                wait(pe, gate_copied, u)
                for q in range(Q):
                    last = pe.transpose(ps_c[0:2 * E, q * P:(q + 1) * P], v.gate_hl[:, q, :], ident[:, :])
                last.then_inc(gate_turned, 1)

            def body(c, p, s, u, last):
                known = isinstance(u, int)
                if known and u == 0:
                    pe.wait_ge(l_lo_done, 1)
                elif known and s == 0 and p == 0:
                    pe.wait_ge(l_lo_done, NC * (c + 1))
                pe.wait_ge(x_lo_done, 2 * u + 1)
                wait(pe, acc_copied, u - 1)
                propagate(c, s, u, 0, range(0, Q))
                if not (known and u < 2):
                    turn_gate(u - 2)
                if not (known and u < 1):
                    project(u - 1)
                if known and u == 0:
                    pe.wait_ge(l_lo_done, 2)
                propagate(c, s, u, 0, range(Q, HB))
                pe.wait_ge(x_lo_done, 2 * u + 2)
                if known and u == 0:
                    pe.wait_ge(l_lo_done, 3)
                propagate(c, s, u, 1, range(0, Q))
                if not (known and u < 1):
                    turn_z(u - 1)
                if known and u == 0:
                    pe.wait_ge(l_lo_done, 4)
                propagate(c, s, u, 1, range(Q, HB))
                if not (known and u < 1):
                    route(u - 1)

            over_units(pe, body)
            turn_gate(U - 2)
            project(U - 1)
            turn_z(U - 1)
            route(U - 1)
            turn_gate(U - 1)

        @block.scalar
        def _(act):
            def l_high(c, r):
                act.wait_ge(l_made, NC * c + r + 1)
                if c >= 2:
                    act.wait_ge(half_used, 2 * B * (c - 1))
                act.activation(v.l_hi[c % 2][:, bass.ds(r * Q, Q), :], v.s_st[:, :, :], ACT.Copy).then_inc(l_hi_done, 1)

            def x_high(u, half, s):
                act.wait_ge(xn_loaded[half], 32 * u + 32)
                wait(act, half_used, 2 * u + half - 1)
                act.activation(v.x_hi[half][:, :, :], v.xn_in[half][:, :, :], ACT.Copy).then_inc(x_hi_done, 1)

            def copy_acc(u, s):
                act.wait_ge(half_used, 2 * u + 2)
                wait(act, w_done, u)
                act.activation(v.y_t[:, :], acc[s][:, :], ACT.Copy).then_inc(acc_copied, 1)

            def copy_z(u):
                act.wait_ge(zt_done, u + 1)
                wait(act, logits_done, u)
                wait(act, z_lo_done, u)
                act.activation(v.z_t[:, :], ps_z[:, :], ACT.Copy).then_inc(z_t_done, 1)
                wait(act, z_stored, 16 * u)
                act.wait_ge(z_t_done, u + 1)
                act.activation(v.z_hl[:, 0, :], v.z_t[:, :], ACT.Copy).then_inc(z_hi_done, 1)

            def copy_gate(u):
                act.wait_ge(gate_turned, u + 1)
                wait(act, gate_stored, 16 * u)
                act.activation(v.gate_t[:, :], ps_c[0:2 * E, :], ACT.Copy).then_inc(gate_copied, 1)
                act.wait_ge(gate_copied, u + 1)
                act.dma_start(v.c_dram[bass.ds(u, 1)].rearrange("a e n -> (a e) n"), v.gate_t[:, :]).then_inc(gate_stored, 16)

            def store_z(u):
                act.wait_ge(res_done, u + 1)
                act.dma_start(v.res_dram[bass.ds(u, 1)].rearrange("a p n -> (a p) n"),
                              v.res[:, :, :].rearrange("p q f -> p (q f)")).then_inc(res_stored, 16)
                act.wait_ge(z_hi_done, u + 1)
                act.wait_ge(z_lo_done, u + 1)
                act.dma_start(v.z_dram[bass.ds(u, 1)].rearrange("a p h n -> (a p) h n"),
                              v.z_hl[:, :, :].bitcast(FP32)).then_inc(z_stored, 16)

            def exps(u):
                act.wait_ge(shift_done, u + 1)
                act.activation(v.expo[:, :, :], v.shifted[:, :, :], ACT.Exp).then_inc(exp_done, 1)

            l_high(0, 0)
            x_high(0, 0, 0)
            l_high(0, 1)
            l_high(0, 2)

            def body(c, p, s, u, last):
                known = isinstance(u, int)
                x_high(u, 1, s)
                if known and u == 0:
                    l_high(0, 3)
                if not (known and u < 2):
                    exps(u - 2)
                if not (known and u < 2):
                    copy_gate(u - 2)
                if s == 1 and c + 1 < NC:
                    l_high(c + 1, p)
                if not (known and u < 1):
                    copy_z(u - 1)
                if not last:
                    x_high(u + 1, 0, 1 - s)
                if not (known and u < 1):
                    store_z(u - 1)
                copy_acc(u, s)

            over_units(act, body)
            exps(U - 2)
            copy_gate(U - 2)
            copy_z(U - 1)
            store_z(U - 1)
            exps(U - 1)
            copy_gate(U - 1)
            act.wait_ge(gate_stored, 16 * U)
            act.wait_ge(res_stored, 16 * U)
            act.wait_ge(z_stored, 16 * U)

        @block.gpsimd
        def _(pool):
            def l_low(c, r):
                pool.wait_ge(l_hi_done, NC * c + r + 1)
                pool.tensor_tensor(out=v.l_lo[c % 2][:, bass.ds(r * Q, Q), :], in0=v.s_st[:, :, :],
                                   in1=v.l_hi[c % 2][:, bass.ds(r * Q, Q), :].bitcast(FP32),
                                   op=ALU.subtract).then_inc(l_lo_done, 1)

            def x_low(u, half):
                pool.wait_ge(x_hi_done, 2 * u + half + 1)
                pool.tensor_tensor(out=v.x_lo[half][:, :, :], in0=v.xn_in[half][:, :, :],
                                   in1=v.x_hi[half][:, :, :].bitcast(FP32), op=ALU.subtract).then_inc(x_lo_done, 1)

            def rstds(u):
                pool.wait_ge(var_done, u + 1)
                pool.tensor_tensor(out=v.rstd[:, :], in0=v.var_eps[:, :], in1=v.neg_half[:, 0:Q],
                                   op=ALU.pow).then_inc(rstd_done, 1)

            l_low(0, 0)
            x_low(0, 0)
            l_low(0, 1)
            l_low(0, 2)

            def body(c, p, s, u, last):
                known = isinstance(u, int)
                x_low(u, 1)
                if known and u == 0:
                    l_low(0, 3)
                if not (known and u < 1):
                    rstds(u - 1)
                if s == 1 and c + 1 < NC:
                    l_low(c + 1, p)
                if not last:
                    x_low(u + 1, 0)

            over_units(pool, body)
            rstds(U - 1)

        @block.vector
        def _(dve):
            def make_l(c, r):
                dve.wait_ge(s_loaded, 16 * (NC * c + r + 1))
                diagonal = isinstance(r, int) and r == 0
                for j in range(Q):
                    last = dve.scalar_tensor_tensor(
                        out=v.s_st[:, j, :], in0=v.s_st[:, j, :], scalar=v.d_col[:, bass.ds((r + c) * Q + j, 1)],
                        in1=v.d_row[:, c * CW:(c + 1) * CW], op0=ALU.mult, op1=ALU.mult)
                if diagonal:
                    last.then_inc(l_scaled, 1)
                    dve.wait_ge(l_scaled, c + 1)
                    for j in range(Q):
                        part = v.s_st[:, j, j * P:(j + 1) * P]
                        last = dve.tensor_tensor(out=part, in0=part, in1=ident[:, :], op=ALU.add)
                last.then_inc(l_made, 1)

            def mid(u):
                dve.wait_ge(w_done, u + 1)
                dve.wait_ge(x_res_in, 16 * u + 16)
                wait(dve, res_done, u)
                dve.scalar_tensor_tensor(out=v.x1[:, :, :].rearrange("p q f -> p (q f)"), in0=ps_w[:, :], scalar=0.0,
                                         in1=v.x_res[:, :, :].rearrange("p q f -> p (q f)"),
                                         op0=ALU.max, op1=ALU.add).then_inc(x1_done, 1)
                dve.wait_ge(x1_done, u + 1)
                for q in range(Q):
                    last = dve.bn_stats(out=v.stats[:, q, :], in_=v.x1[:, q, :])
                dve.drain()
                for q in range(Q):
                    last = dve.bn_aggr(out=v.mv[:, q, :], in_=v.stats[:, q, :])
                last.then_inc(mv_done, 1)
                dve.wait_ge(mv_done, u + 1)
                dve.tensor_scalar(v.var_eps[:, :], v.mv[:, :, 1], v.EPS, None, ALU.add).then_inc(var_done, 1)
                dve.wait_ge(rstd_done, u + 1)
                wait(dve, zt_done, u)
                for q in range(Q):
                    last = dve.tensor_scalar(v.z[:, q, :], v.x1[:, q, :], v.mv[:, q, 0:1], v.rstd[:, q:q + 1],
                                             ALU.subtract, ALU.mult)
                last.then_inc(z_done, 1)
                dve.wait_ge(z_done, u + 1)
                wait(dve, res_stored, 16 * u)
                dve.tensor_tensor(out=v.res[:, :, :], in0=v.x1[:, :, :], in1=v.z[:, :, :], op=ALU.add).then_inc(res_done, 1)

            def z_low(u):
                dve.wait_ge(z_hi_done, u + 1)
                dve.tensor_tensor(out=v.z_hl[:, 1, :], in0=v.z_t[:, :], in1=v.z_hl[:, 0, :].bitcast(FP32),
                                  op=ALU.subtract).then_inc(z_lo_done, 1)

            def gates_first(u):
                dve.wait_ge(logits_done, u + 1)
                logits = v.logits
                dve.tensor_copy(logits[:, :, :].rearrange("p q e -> p (q e)"), ps_r[:, 0:Q * E]).then_inc(logits_copied, 1)
                dve.drain()
                for q in range(Q):
                    dve.max(out=v.top_val[:, q, :], in_=logits[:, q, :])
                dve.drain()
                for q in range(Q):
                    last = dve.max_index(out=v.top_idx[:, q, :], in_max=v.top_val[:, q, :], in_values=logits[:, q, :])
                last.then_inc(idx_done, 1)
                wait(dve, exp_done, u)
                dve.tensor_tensor(out=v.shifted[:, :, :], in0=logits[:, :, :], in1=v.top_val[:, :, 0:1].to_broadcast([P, Q, E]),
                                  op=ALU.subtract).then_inc(shift_done, 1)

            def gates_second(u):
                first = ROUTE_STEPS * u
                dve.wait_ge(idx_done, u + 1)
                dve.tensor_copy(v.top_idx_f[:, :, :], v.top_idx[:, :, 0:2]).then_inc(route_step, 1)
                dve.wait_ge(route_step, first + 1)
                for n, chosen in enumerate((v.is_1st, v.is_2nd)):
                    dve.tensor_tensor(out=chosen[:, :, :], in0=v.iota_e[:, :, :],
                                      in1=v.top_idx_f[:, :, n:n + 1].to_broadcast([P, Q, E]),
                                      op=ALU.is_equal).then_inc(route_step, 1)
                dve.wait_ge(route_step, first + 3)
                dve.tensor_tensor(out=v.is_top[:, :, :], in0=v.is_1st[:, :, :], in1=v.is_2nd[:, :, :],
                                  op=ALU.add).then_inc(route_step, 1)
                dve.wait_ge(exp_done, u + 1)
                dve.tensor_reduce(out=v.sum_all[:, :], in_=v.expo[:, :, :], axis=AX.X, op=ALU.add)
                dve.wait_ge(route_step, first + 4)
                dve.tensor_tensor(out=v.picked[:, :, :], in0=v.expo[:, :, :], in1=v.is_top[:, :, :],
                                  op=ALU.mult).then_inc(route_step, 1)
                dve.wait_ge(route_step, first + 5)
                dve.tensor_reduce(out=v.sum_top[:, :], in_=v.picked[:, :, :], axis=AX.X, op=ALU.add).then_inc(route_step, 1)
                dve.wait_ge(route_step, first + 6)
                dve.scalar_tensor_tensor(out=v.guarded[:, :], in0=v.sum_all[:, :], scalar=1e-12, in1=v.sum_top[:, :],
                                         op0=ALU.mult, op1=ALU.max).then_inc(route_step, 1)
                dve.wait_ge(route_step, first + 7)
                dve.reciprocal(v.inv_top[:, :], v.guarded[:, :]).then_inc(route_step, 1)
                dve.wait_ge(route_step, first + 8)
                dve.tensor_tensor(out=v.gate[:, :, :], in0=v.picked[:, :, :],
                                  in1=v.inv_top[:, :, None].to_broadcast([P, Q, E]), op=ALU.mult).then_inc(gate_step, 1)
                dve.wait_ge(gate_step, 2 * u + 1)
                wait(dve, gate_turned, u)
                dve.tensor_copy(v.gate_hl[:, :, 0:E].bitcast(FP32R), v.gate[:, :, :]).then_inc(gate_step, 1)
                dve.wait_ge(gate_step, 2 * u + 2)
                dve.tensor_tensor(out=v.gate_hl[:, :, E:2 * E].bitcast(FP32R), in0=v.gate[:, :, :],
                                  in1=v.gate_hl[:, :, 0:E], op=ALU.subtract).then_inc(gate_done, 1)

            for r in range(NC):
                make_l(0, r)

            def body(c, p, s, u, last):
                known = isinstance(u, int)
                if not (known and u < 2):
                    gates_second(u - 2)
                if not (known and u < 1):
                    mid(u - 1)
                    z_low(u - 1)
                if s == 0 and c + 1 < NC:
                    make_l(c + 1, p)
                if not (known and u < 1):
                    gates_first(u - 1)

            over_units(dve, body)
            gates_second(U - 2)
            mid(U - 1)
            z_low(U - 1)
            gates_first(U - 1)
            gates_second(U - 1)


def build_experts(nc, sem, v):
    B, E, CW, NC, Q, U, PAIRS, R = v.B, v.E, v.CW, v.NC, v.Q, v.U, v.PAIRS, v.R
    T = E * U
    ps_h = [v.banks[0], v.banks[1]]
    ps_g = [v.banks[2], v.banks[3]]
    ps_o = [v.banks[4], v.banks[5]]
    ps_t = v.banks[6]
    LAG = 2

    consts_made = sem("e_consts_made")
    weights_in = [sem(f"weights_in{i}") for i in range(2)]
    b2_in = sem("b2_in")
    w_hi_made = sem("w_hi_made")
    w_lo_made = sem("w_lo_made")
    c_cleared = sem("c_cleared")
    z_in = [sem(f"z_in{i}") for i in range(2)]
    c_in = [sem(f"c_in{i}") for i in range(2)]
    r_in = [sem(f"r_in{i}") for i in range(2)]
    h_done = sem("h_done")
    g_done = sem("g_done")
    gelu_done = sem("gelu_done")
    gated_done = sem("gated_done")
    hi_done = sem("hi_done")
    lo_done = sem("lo_done")
    o_done = sem("o_done")
    ot_copied = sem("ot_copied")
    o_turned = sem("o_turned")
    fin_done = sem("fin_done")
    stored = [sem(f"stored{i}") for i in range(2)]

    def over_units(eng, body):
        for s in range(2):
            body(0, s, s)
        with eng.Fori(1, U // 2) as h:
            for s in range(2):
                body(h, s, 2 * h + s)

    with nc.Block() as block:

        @block.sync
        def _(sp):
            sp.dma_start(v.w_raw[:, 0, :, :], v.w1.rearrange("e d h -> d e h")).then_inc(weights_in[0], 16)
            sp.dma_start(v.w_raw[:, 1, :, :], v.w2.rearrange("e h d -> h e d")).then_inc(weights_in[1], 16)
            sp.wait_ge(consts_made, 3)
            for half in range(2):
                sp.dma_start(v.b2_raw[half * E:(half + 1) * E, :], v.b2).then_inc(b2_in, 16)
            sp.wait_ge(c_cleared, 2)

            def body(h, s, u):
                if not isinstance(u, int):
                    u = sp.snap(u)
                wait(sp, h_done, E * (u - 1) if isinstance(u, int) else E * u - E)
                sp.dma_start(v.z_e[s][:, :, :].bitcast(FP32),
                             v.z_dram[bass.ds(u, 1)].rearrange("a p h n -> (a p) h n")).then_inc(z_in[s], 16)
                wait(sp, o_done, E * (u - 1) - E + 1 if isinstance(u, int) else E * u - 2 * E + 1)
                wait(sp, g_done, E * (u - 1) if isinstance(u, int) else E * u - E)
                sp.dma_start(v.c_e[s][0:2 * E, :].bitcast(FP32),
                             v.c_dram[bass.ds(u, 1)].rearrange("a e n -> (a e) n")).then_inc(c_in[s], 16)
                wait(sp, fin_done, u - 1)
                sp.dma_start(v.r_e[s][:, :],
                             v.res_dram[bass.ds(u, 1)].rearrange("a p n -> (a p) n")).then_inc(r_in[s], 16)

            over_units(sp, body)

        @block.gpsimd
        def _(pool):
            pool.memset(v.pick_raw[:, :, :], 0.0).then_inc(consts_made, 1)
            pool.memset(v.c_zero[:, :], 0.0).then_inc(consts_made, 1)
            pool.memset(v.b2_raw[:, :], 0.0).then_inc(consts_made, 1)
            for half in range(2):
                pool.wait_ge(consts_made, 3 + half)
                pool.affine_select(out=v.pick_raw[:, :, :], in_=v.pick_raw[:, :, :], compare_op=ALU.not_equal,
                                   fill=1.0, base=-half * E, pattern=[[-1, E], [0, P]],
                                   channel_multiplier=1).then_inc(consts_made, 1)

            def store(h, s, u):
                pool.wait_ge(fin_done, u + 1)
                if isinstance(u, int):
                    b, n = u % B, u // B * CW
                else:
                    b, n = u & (B - 1), (u // B) * CW
                rows = v.out[bass.ds(b, 1)][:, bass.ds(n, CW), :]
                pool.dma_start(rows.rearrange("a (q p) f -> p (a q) f", p=P),
                               v.fin[s][:, :].rearrange("p (q f) -> p q f", f=P)).then_inc(stored[s], 16)

            over_units(pool, store)
            for s in range(2):
                pool.wait_ge(stored[s], 16 * (U // 2))

        @block.tensor
        def _(pe):
            def up_product(s, u, e):
                t = E * u + e
                k = e % 2
                if e == 0:
                    pe.wait_ge(z_in[s], 8 * u + (16 - 8 * s))
                    pe.wait_ge(c_in[s], 8 * u + (16 - 8 * s))
                wait(pe, gelu_done, t - 1)
                pe.matmul(ps_h[k][:, :], v.w1_hi[:, e, :], v.z_e[s][:, 0, :], start=True, stop=False)
                pe.matmul(ps_h[k][:, :], v.w1_hi[:, e, :], v.z_e[s][:, 1, :], start=False, stop=False)
                pe.matmul(ps_h[k][:, :], v.w1_lo[:, e, :], v.z_e[s][:, 0, :], start=False, stop=True).then_inc(h_done, 1)
                wait(pe, gated_done, t - 1)
                pe.matmul(ps_g[k][:, :], v.pick[:, e, :], v.c_e[s][:, :], start=True, stop=True).then_inc(g_done, 1)

            def down_product(s, u, e):
                t = E * u + e
                if e == 0:
                    wait(pe, ot_copied, u - 1)
                    pe.matmul(ps_o[s][:, :], v.b2_hi[:, :], v.c_e[s][:, :], start=True, stop=False)
                    pe.matmul(ps_o[s][:, :], v.b2_lo[:, :], v.c_e[s][:, :], start=False, stop=False)
                pe.wait_ge(lo_done, t + 1)
                hi, lo = v.g_hi[e % R], v.g_lo[e % R]
                pe.matmul(ps_o[s][:, :], v.w2_hi[:, e, :], hi[:, :], start=False, stop=False)
                pe.matmul(ps_o[s][:, :], v.w2_hi[:, e, :], lo[:, :], start=False, stop=False)
                pe.matmul(ps_o[s][:, :], v.w2_lo[:, e, :], hi[:, :], start=False, stop=(e == E - 1)).then_inc(o_done, 1)

            def turn_out(u):
                pe.wait_ge(ot_copied, u + 1)
                wait(pe, fin_done, u)
                for q in range(Q):
                    last = pe.transpose(ps_t[:, q * P:(q + 1) * P], v.o_t[:, q * P:(q + 1) * P], v.ident[:, :])
                last.then_inc(o_turned, 1)

            pe.wait_ge(w_hi_made, 4)
            pe.wait_ge(w_lo_made, 3)

            def body(h, s, u):
                known = isinstance(u, int)
                for e in range(E):
                    up_product(s, u, e)
                    if e >= LAG:
                        down_product(s, u, e - LAG)
                    elif not (known and u == 0):
                        down_product(1 - s, u - 1, E + e - LAG)
                    if e == 4 and not (known and u == 0):
                        turn_out(u - 1)

            over_units(pe, body)
            for e in range(E - LAG, E):
                down_product(1, U - 1, e)
            turn_out(U - 1)

        @block.scalar
        def _(act):
            for i, half in enumerate((v.w1_hi, v.w2_hi)):
                act.wait_ge(weights_in[i], 16)
                act.activation(half[:, :, :], v.w_raw[:, i, :, :], ACT.Copy).then_inc(w_hi_made, 1)
            act.wait_ge(b2_in, 32)
            act.activation(v.b2_hi[:, :], v.b2_raw[:, :], ACT.Copy).then_inc(w_hi_made, 1)
            act.wait_ge(consts_made, 5)
            act.activation(v.pick[:, :, :], v.pick_raw[:, :, :], ACT.Copy).then_inc(w_hi_made, 1)

            def gelu(u, e):
                t = E * u + e
                act.wait_ge(h_done, t + 1)
                wait(act, gated_done, t - R + 1)
                act.activation(v.act_h[e % R][:, :], ps_h[e % 2][:, :], ACT.Gelu,
                               bias=v.b1_sb[:, e:e + 1]).then_inc(gelu_done, 1)

            def high(u, e):
                t = E * u + e
                act.wait_ge(gated_done, t + 1)
                wait(act, o_done, t - R + 1)
                act.activation(v.g_hi[e % R][:, :], v.gated[e % R][:, :], ACT.Copy).then_inc(hi_done, 1)

            def copy_out(u, s):
                act.wait_ge(o_done, E * u + E)
                wait(act, o_turned, u)
                act.activation(v.o_t[:, :], ps_o[s][:, :], ACT.Copy).then_inc(ot_copied, 1)

            def body(h, s, u):
                known = isinstance(u, int)
                for e in range(E):
                    gelu(u, e)
                    if e >= 1:
                        high(u, e - 1)
                    elif not (known and u == 0):
                        high(u - 1, E - 1)
                    if e == 3 and not (known and u == 0):
                        copy_out(u - 1, 1 - s)

            over_units(act, body)
            high(U - 1, E - 1)
            copy_out(U - 1, 1)

        @block.vector
        def _(dve):
            dve.wait_ge(consts_made, 5)
            for s in range(2):
                dve.tensor_copy(v.c_e[s][:, :], v.c_zero[:, :]).then_inc(c_cleared, 1)
            for i, (hi, lo) in enumerate(((v.w1_hi, v.w1_lo), (v.w2_hi, v.w2_lo))):
                dve.wait_ge(w_hi_made, i + 1)
                dve.tensor_tensor(out=lo[:, :, :], in0=v.w_raw[:, i, :, :], in1=hi[:, :, :].bitcast(FP32),
                                  op=ALU.subtract).then_inc(w_lo_made, 1)
            dve.wait_ge(w_hi_made, 3)
            dve.tensor_tensor(out=v.b2_lo[:, :], in0=v.b2_raw[:, :], in1=v.b2_hi[:, :].bitcast(FP32),
                              op=ALU.subtract).then_inc(w_lo_made, 1)

            def scale(u, e):
                t = E * u + e
                dve.wait_ge(gelu_done, t + 1)
                dve.wait_ge(g_done, t + 1)
                wait(dve, hi_done, t - R + 1)
                dve.tensor_tensor(out=v.gated[e % R][:, :], in0=ps_g[e % 2][:, :], in1=v.act_h[e % R][:, :],
                                  op=ALU.mult).then_inc(gated_done, 1)

            def low(u, e):
                dve.wait_ge(hi_done, E * u + e + 1)
                dve.tensor_tensor(out=v.g_lo[e % R][:, :], in0=v.gated[e % R][:, :],
                                  in1=v.g_hi[e % R][:, :].bitcast(FP32), op=ALU.subtract).then_inc(lo_done, 1)

            def finish(u, s):
                dve.wait_ge(o_turned, u + 1)
                dve.wait_ge(r_in[s], 8 * u + (16 - 8 * s))
                wait(dve, stored[s], 8 * u - 8 * s)
                dve.tensor_tensor(out=v.fin[s][:, :], in0=ps_t[:, :], in1=v.r_e[s][:, :], op=ALU.add).then_inc(fin_done, 1)

            def body(h, s, u):
                known = isinstance(u, int)
                for e in range(E):
                    scale(u, e)
                    if e >= 1:
                        low(u, e - 1)
                    elif not (known and u == 0):
                        low(u - 1, E - 1)
                    if e == 6 and not (known and u == 0):
                        finish(u - 1, 1 - s)

            over_units(dve, body)
            low(U - 1, E - 1)
            finish(U - 1, 1)


_INS = ["x", "adj", "L0_gnn_W", "L0_ffn_router_w", "L0_ffn_w1", "L0_ffn_b1", "L0_ffn_w2", "L0_ffn_b2"]


def kernel(**inputs):
    import numpy as np
    import concourse.bacc as bacc
    from concourse.bass_utils import run_bass_kernel_spmd

    nc = bacc.Bacc("TRN2", target_bir_lowering=False, num_devices=1)
    arrays, args = {}, []
    for name in _INS:
        a = np.ascontiguousarray(inputs[name])
        arrays[f"in_{name}"] = a
        args.append(nc.dram_tensor(f"in_{name}", a.shape, mybir.dt.from_np(a.dtype), kind="ExternalInput").ap())
    args.append(nc.dram_tensor("out", inputs["x"].shape, FP32, kind="ExternalOutput").ap())
    gnn_moe_kernel(nc, *args)
    r = run_bass_kernel_spmd(nc, [arrays], core_ids=[0])
    return r.results[0]["out"]
```

```python
import concourse.bass as bass
from concourse import mybir
from contextlib import ExitStack

FP32 = mybir.dt.float32
FP32R = mybir.dt.float32r
U32 = mybir.dt.uint32
ALU = mybir.AluOpType
ACT = mybir.ActivationFunctionType
AX = mybir.AxisListType

P = 128


class Plan:
    pass


def gnn_moe_kernel(nc, x, adj, gnn_w, router_w, w1, b1, w2, b2, out):
    B, N, D = x.shape
    E = router_w.shape[0]
    MB = N // P
    CW = 512
    NC = N // CW
    Q = CW // P
    U = NC * B
    PAIRS = B // 2
    v = Plan()
    v.x, v.adj, v.gnn_w, v.router_w, v.w1, v.b1, v.w2, v.b2, v.out = x, adj, gnn_w, router_w, w1, b1, w2, b2, out
    v.B, v.N, v.D, v.E, v.MB, v.CW, v.NC, v.Q, v.U, v.PAIRS = B, N, D, E, MB, CW, NC, Q, U, PAIRS
    v.EPS = 1e-5
    assert D == P and N % CW == 0 and B % 2 == 0 and E == 8 and PAIRS == NC

    v.s_dram = nc.dram_tensor("s_scratch", (NC, P, MB, CW), FP32, kind="Internal").ap()
    v.xn_dram = nc.dram_tensor("xn_scratch", (B, P, MB, D), FP32, kind="Internal").ap()
    v.z_dram = nc.dram_tensor("z_scratch", (U, P, 2, CW), FP32, kind="Internal").ap()
    v.c_dram = nc.dram_tensor("c_scratch", (U, 2 * E, CW), FP32, kind="Internal").ap()
    v.res_dram = nc.dram_tensor("res_scratch", (U, P, CW), FP32, kind="Internal").ap()

    ctx = ExitStack()
    with ctx:
        limit = nc.sbuf_usable_end
        cursor = [nc.sbuf_base]

        def sb(name, shape, dt, at=None):
            c = cursor if at is None else at
            size = 4
            for n in shape[1:]:
                size *= n
            c[0] = (c[0] + 63) // 64 * 64
            t = nc.alloc_sbuf_tensor_at(name, shape, dt, offset=c[0])
            c[0] += size
            return t

        def sem(name):
            return ctx.enter_context(nc.semaphore(name))

        v.banks = [ctx.enter_context(nc.psum_tensor(f"bank{i}", [P, 512], FP32)) for i in range(8)]

        v.ident = sb("ident", [P, P], FP32)
        v.ones = sb("ones", [P, P], FP32)
        v.neg_half = sb("neg_half", [P, MB], FP32)
        v.iota_e = sb("iota_e", [P, Q, E], FP32)
        v.gnn_w_sb = sb("gnn_w_sb", [P, P], FP32)
        v.rwt_sb = sb("rwt_sb", [P, E], FP32)
        v.b1_sb = sb("b1_sb", [P, E], FP32)
        v.d_row = sb("d_row", [P, N], FP32)
        v.d_col = sb("d_col", [P, 2 * MB], FP32)
        base = cursor[0]

        at = [base]
        v.l_hi, v.l_lo, region = [None] * 2, [None] * 2, []
        for i in range(2):
            region.append(at[0])
            v.l_hi[i] = sb(f"l_hi{i}", [P, MB, CW], FP32R, at)
            region.append(at[0])
            v.l_lo[i] = sb(f"l_lo{i}", [P, MB, CW], FP32R, at)
        region.append(at[0])
        v.s_st = sb("s_st", [P, Q, CW], FP32, at)
        v.xn_in = [sb(f"xn_in{i}", [P, MB // 2, P], FP32, at) for i in range(2)]
        v.x_hi = [sb(f"x_hi{i}", [P, MB // 2, P], FP32R, at) for i in range(4)]
        v.x_lo = [sb(f"x_lo{i}", [P, MB // 2, P], FP32R, at) for i in range(4)]
        v.x_res = sb("x_res", [P, Q, P], FP32, at)
        v.y_t = sb("y_t", [P, CW], FP32, at)
        v.x1 = sb("x1", [P, Q, P], FP32, at)
        v.z = sb("z", [P, Q, P], FP32, at)
        v.res = sb("res", [P, Q, P], FP32, at)
        v.z_t = sb("z_t", [P, CW], FP32, at)
        v.z_hl = sb("z_hl", [P, 2, CW], FP32R, at)
        v.stats = sb("stats", [P, Q, 6], FP32, at)
        v.mv = sb("mv", [P, Q, 2], FP32, at)
        v.var_eps = sb("var_eps", [P, Q], FP32, at)
        v.rstd = sb("rstd", [P, Q], FP32, at)
        v.logits = sb("logits", [P, Q, E], FP32, at)
        v.top_val = sb("top_val", [P, Q, 8], FP32, at)
        v.top_idx = sb("top_idx", [P, Q, 8], U32, at)
        v.top_idx_f = sb("top_idx_f", [P, Q, 2], FP32, at)
        v.shifted = sb("shifted", [P, Q, E], FP32, at)
        v.expo = sb("expo", [P, Q, E], FP32, at)
        v.is_1st = sb("is_1st", [P, Q, E], FP32, at)
        v.is_2nd = sb("is_2nd", [P, Q, E], FP32, at)
        v.is_top = sb("is_top", [P, Q, E], FP32, at)
        v.picked = sb("picked", [P, Q, E], FP32, at)
        v.sum_all = sb("sum_all", [P, Q], FP32, at)
        v.sum_top = sb("sum_top", [P, Q], FP32, at)
        v.guarded = sb("guarded", [P, Q], FP32, at)
        v.inv_top = sb("inv_top", [P, Q], FP32, at)
        v.gate = sb("gate", [P, Q, E], FP32, at)
        v.gate_hl = sb("gate_hl", [P, Q, 2 * E], FP32, at)
        v.gate_t = sb("gate_t", [2 * E, CW], FP32, at)
        v.x_stats = sb("x_stats", [P, MB, 6], FP32, at)
        v.x_mv = sb("x_mv", [P, MB, 2], FP32, at)
        v.x_var = sb("x_var", [P, MB], FP32, at)
        v.x_rstd = sb("x_rstd", [P, MB], FP32, at)
        v.x_shift = sb("x_shift", [P, MB], FP32, at)
        assert at[0] <= limit, at

        at = [region[0]]
        v.low = [sb(f"low{i}", [P, N], FP32, at) for i in range(3)]
        v.up = [sb(f"up{i}", [P, MB - 1, P], FP32, at) for i in range(3)]
        v.total = [sb(f"total{i}", [P, CW], FP32, at) for i in range(4)]
        assert at[0] <= region[2] - Q * CW * 4, at
        at = [region[2] - Q * CW * 4]
        v.s_low = [sb("s_low0", [P, N - CW], FP32, at), None]
        at = [region[2]]
        v.s0 = sb("s0", [P, MB, CW], FP32, at)
        v.s_low[1] = sb("s_low1", [P, N - CW], FP32, at)
        v.s_up = [sb(f"s_up{i}", [P, MB - 1, P], FP32, at) for i in range(2)]
        assert at[0] <= region[4] - Q * CW * 4, at
        v.x_raw = [sb("x_raw0", [P, MB, P], FP32, [region[4] - Q * CW * 4]),
                   sb("x_raw1", [P, MB, P], FP32, [region[3] - Q * CW * 4])]
        at = [region[4]]
        v.deg_low = sb("deg_low", [P, MB, NC], FP32, at)
        v.deg_up = sb("deg_up", [P, MB, MB], FP32, at)
        v.deg_parts = sb("deg_parts", [P, 2, MB], FP32, at)
        v.deg = sb("deg", [P, MB], FP32, at)
        v.deg_pos = sb("deg_pos", [P, MB], FP32, at)
        v.deg_safe = sb("deg_safe", [P, MB], FP32, at)
        v.deg_root = sb("deg_root", [P, MB], FP32, at)
        v.d_inv = sb("d_inv", [P, MB], FP32, at)
        v.diag_d = sb("diag_d", [P, Q, P], FP32, at)
        assert at[0] <= region[4] + Q * CW * 4, at

        at = [base]
        v.w_raw = sb("w_raw", [P, 2, E, P], FP32, at)
        v.b2_raw = sb("b2_raw", [P, P], FP32, at)
        v.pick_raw = sb("pick_raw", [P, E, P], FP32, at)
        v.w1_hi = sb("w1_hi", [P, E, P], FP32R, at)
        v.w1_lo = sb("w1_lo", [P, E, P], FP32R, at)
        v.w2_hi = sb("w2_hi", [P, E, P], FP32R, at)
        v.w2_lo = sb("w2_lo", [P, E, P], FP32R, at)
        v.b2_hi = sb("b2_hi", [P, P], FP32R, at)
        v.b2_lo = sb("b2_lo", [P, P], FP32R, at)
        v.pick = sb("pick", [P, E, P], FP32R, at)
        v.z_e = [sb(f"z_e{i}", [P, 2, CW], FP32R, at) for i in range(2)]
        v.c_e = [sb(f"c_e{i}", [P, CW], FP32R, at) for i in range(2)]
        v.c_zero = sb("c_zero", [P, CW], FP32, at)
        v.r_e = [sb(f"r_e{i}", [P, CW], FP32, at) for i in range(2)]
        R = v.R = 4
        v.act_h = [sb(f"act_h{i}", [P, CW], FP32, at) for i in range(R)]
        v.gated = [sb(f"gated{i}", [P, CW], FP32, at) for i in range(R)]
        v.g_hi = [sb(f"g_hi{i}", [P, CW], FP32R, at) for i in range(R)]
        v.g_lo = [sb(f"g_lo{i}", [P, CW], FP32R, at) for i in range(R)]
        v.o_t = sb("o_t", [P, CW], FP32, at)
        v.fin = [sb(f"fin{i}", [P, CW], FP32, at) for i in range(2)]
        assert at[0] <= limit, at

        setup, graph = setup_stage(nc, sem, v), graph_stage(nc, sem, v)
        with nc.Block() as block:

            @block.sync
            def _(sp):
                setup.sync(sp)
                graph.sync(sp)

            @block.gpsimd
            def _(pool):
                setup.gpsimd(pool)
                graph.gpsimd(pool)

            @block.tensor
            def _(pe):
                setup.tensor(pe)
                graph.tensor(pe)

            @block.scalar
            def _(act):
                setup.scalar(act)
                graph.scalar(act)

            @block.vector
            def _(dve):
                setup.vector(dve)
                graph.vector(dve)

        build_experts(nc, sem, v)


def ln_program(nc, sem, v):
    B, MB, EPS = v.B, v.MB, v.EPS
    HB = MB // 2
    ln = Plan()
    ln.loaded = [sem(f"ln_loaded{i}") for i in range(4)]
    ln.mv_done = sem("ln_mv_done")
    ln.var_done = sem("ln_var_done")
    ln.rstd_done = sem("ln_rstd_done")
    ln.shift_done = sem("ln_shift_done")
    ln.done = sem("ln_done")
    ln.x_hi_done = sem("x_hi_done")
    ln.x_lo_done = sem("x_lo_done")
    ln.stored = [sem(f"ln_stored{i}") for i in range(2)]

    def loads_until(b, s):
        if isinstance(b, int) and b < 2:
            return 16 * (b + 1)
        return 8 * b + 32 if s == 0 else 8 * b - 8

    def statistics(dve, b, half, s):
        n = 2 * b + half
        raw = 0 if isinstance(b, int) and b < 2 else s
        ms = range(half * HB, (half + 1) * HB)
        dve.wait_ge(ln.loaded[2 * raw + half], loads_until(b, s))
        for m in ms:
            dve.bn_stats(out=v.x_stats[:, m, :], in_=v.x_raw[raw][:, m, :])
        dve.drain()
        for m in ms:
            last = dve.bn_aggr(out=v.x_mv[:, m, :], in_=v.x_stats[:, m, :])
        last.then_inc(ln.mv_done, 1)
        dve.wait_ge(ln.mv_done, n + 1)
        dve.tensor_scalar(v.x_var[:, ms[0]:ms[-1] + 1], v.x_mv[:, ms[0]:ms[-1] + 1, 1], EPS, None,
                          ALU.add).then_inc(ln.var_done, 1)

    def root(pool, b, half):
        part = slice(half * HB, (half + 1) * HB)
        pool.wait_ge(ln.var_done, 2 * b + half + 1)
        pool.tensor_tensor(out=v.x_rstd[:, part], in0=v.x_var[:, part], in1=v.neg_half[:, part],
                           op=ALU.pow).then_inc(ln.rstd_done, 1)

    def shift(dve, b, half):
        part = slice(half * HB, (half + 1) * HB)
        dve.wait_ge(ln.rstd_done, 2 * b + half + 1)
        wait(dve, ln.done, 2 * b + half - 1)
        dve.scalar_tensor_tensor(out=v.x_shift[:, part], in0=v.x_mv[:, part, 0], scalar=-1.0, in1=v.x_rstd[:, part],
                                 op0=ALU.mult, op1=ALU.mult).then_inc(ln.shift_done, 1)

    def apply(act, b, half, s):
        raw = 0 if isinstance(b, int) and b < 2 else s
        wait(act, ln.x_lo_done, 2 * b + half - 1)
        if not isinstance(b, int) or b > 0:
            act.wait_ge(ln.stored[half], 16 * b)
        act.wait_ge(ln.shift_done, 2 * b + half + 1)
        for i in range(HB):
            m = half * HB + i
            last = act.activation(v.xn_in[half][:, i, :], v.x_raw[raw][:, m, :], ACT.Identity,
                                  bias=v.x_shift[:, m:m + 1], scale=v.x_rstd[:, m:m + 1])
        last.then_inc(ln.done, 1)

    def load(sp, b, half):
        raw = 0 if b < 2 else b % 2
        if b == 1 or b == 2 or b >= 4:
            before = b - 1 if b <= 2 else b - 2
            sp.wait_ge(ln.done, 2 * before + half + 1)
        rows = v.x[b, half * HB * P:(half + 1) * HB * P, :]
        sp.dma_start(v.x_raw[raw][:, half * HB:(half + 1) * HB, :],
                     rows.rearrange("(m p) f -> p m f", p=P)).then_inc(ln.loaded[2 * raw + half], 16)

    def store(sp, b, half):
        sp.wait_ge(ln.done, 2 * b + half + 1)
        sp.dma_start(v.xn_dram[b, :, half * HB:(half + 1) * HB, :], v.xn_in[half][:, :, :]).then_inc(ln.stored[half], 16)

    def high(act, u, half, s):
        act.activation(v.x_hi[2 * s + half][:, :, :], v.xn_in[half][:, :, :], ACT.Copy).then_inc(ln.x_hi_done, 1)

    def low(pool, u, half, s):
        pool.wait_ge(ln.x_hi_done, 2 * u + half + 1)
        pool.tensor_tensor(out=v.x_lo[2 * s + half][:, :, :], in0=v.xn_in[half][:, :, :],
                           in1=v.x_hi[2 * s + half][:, :, :].bitcast(FP32), op=ALU.subtract).then_inc(ln.x_lo_done, 1)

    ln.high, ln.low = high, low
    ln.statistics, ln.root, ln.shift, ln.apply, ln.load, ln.store = statistics, root, shift, apply, load, store
    return ln


def setup_stage(nc, sem, v):
    B, N, D, E, MB, CW, NC, Q = v.B, v.N, v.D, v.E, v.MB, v.CW, v.NC, v.Q
    low, up, s_low, s_up, s0 = v.low, v.up, v.s_low, v.s_up, v.s0
    ident, ones = v.ident, v.ones
    ln = v.ln = ln_program(nc, sem, v)

    low_in = [sem(f"low_in{i}") for i in range(3)]
    up_in = [sem(f"up_in{i}") for i in range(3)]
    consts_made = v.consts_made = sem("consts_made")
    turned = sem("turned")
    summed = sem("summed")
    relued = sem("relued")
    deg_added = sem("deg_added")
    low_out = [sem(f"low_out{i}") for i in range(2)]
    up_out = [sem(f"up_out{i}") for i in range(2)]
    deg_ready = v.deg_ready = sem("deg_ready")
    safe_step = sem("safe_step")
    root_ready = sem("root_ready")
    diag_ready = sem("diag_ready")
    d_spread = sem("d_spread")
    d_row_ready = v.d_row_ready = sem("d_row_ready")
    small_in = v.small_in = sem("small_in")
    v.small_loads = 3

    def groups(k):
        out = [("low", k, g, Q * g, min(Q, k + 1 - Q * g)) for g in range(k // Q + 1)]
        out += [("up", k, g, Q * g, min(Q, k - Q * g)) for g in range((k + Q - 1) // Q)]
        return out

    every = [g for k in range(MB) for g in groups(k)]
    last_of_step = [sum(len(groups(kk)) for kk in range(k + 1)) for k in range(MB)]
    LNB = 4
    STATS_AFTER, APPLY_AFTER = (5, 9), (7, 11)

    def low_stores(k):
        whole = (k + 1) // Q
        return [(c0, c1) for c0, c1 in ((1, whole), (whole, whole + 1)) if c1 > c0 >= 1 and c0 * Q <= k]

    def stores_before(k, up_to=None):
        same = [kk for kk in range(k % 2, k, 2)]
        return 16 * sum(len(low_stores(kk)) for kk in same), 16 * sum(kk >= Q for kk in same)

    v.s_stores = [(low_out[i], stores_before(MB + i)[0]) for i in range(2)]
    v.s_stores += [(up_out[i], stores_before(MB + i)[1]) for i in range(2)]

    def sync(sp):
        for k in range(MB):
            s = k % 3
            if k >= 3:
                sp.wait_ge(summed, last_of_step[k - 3])
            sp.dma_start(low[s][:, 0:(k + 1) * P], v.adj[k * P:(k + 1) * P, 0:(k + 1) * P]).then_inc(low_in[s], 16)
            if k:
                sp.dma_start(up[s][:, 0:k, :],
                             v.adj[0:k * P, k * P:(k + 1) * P].rearrange("(j p) n -> p j n", p=P)).then_inc(up_in[s], 16)
            if k == 3:
                for half in range(2):
                    ln.load(sp, 0, half)
            if k == APPLY_AFTER[0] + 3:
                for half in range(2):
                    ln.store(sp, 0, half)
                    ln.load(sp, 1, half)
        for half in range(2):
            ln.store(sp, 1, half)
            ln.load(sp, 2, half)

    def gpsimd(pool):
        pool.memset(ident[:, :], 0.0).then_inc(consts_made, 1)
        pool.memset(ones[:, :], 1.0).then_inc(consts_made, 1)
        pool.memset(v.neg_half[:, :], -0.5).then_inc(consts_made, 1)
        for e in range(E):
            pool.memset(v.iota_e[:, :, e:e + 1], float(e)).then_inc(consts_made, 1)
        pool.wait_ge(consts_made, 3 + E)
        pool.affine_select(out=ident[:, :], in_=ident[:, :], compare_op=ALU.not_equal, fill=1.0,
                           base=0, pattern=[[-1, P]], channel_multiplier=1).then_inc(consts_made, 1)
        for b in range(2):
            for half in range(2):
                ln.root(pool, b, half)
            if b == 0:
                for half in range(2):
                    ln.low(pool, 0, half, 0)
        pool.wait_ge(deg_ready, 6)
        pool.tensor_tensor(out=v.deg_root[:, :], in0=v.deg_safe[:, :], in1=v.neg_half[:, :],
                           op=ALU.pow).then_inc(root_ready, 1)

    def scalar(act):
        act.dma_start(v.gnn_w_sb[:, :], v.gnn_w).then_inc(small_in, 16)
        with nc.allow_non_contiguous_dma(reason="small transposed constants"):
            act.dma_start(v.rwt_sb[:, :], v.router_w.rearrange("e d -> d e")).then_inc(small_in, 16)
            act.dma_start(v.b1_sb[:, :], v.b1.rearrange("e h -> h e")).then_inc(small_in, 16)
        for n, (kind, k, g, j0, nj) in enumerate(every):
            act.wait_ge(summed, n + 1)
            owed_low, owed_up = stores_before(k)
            if kind == "low" and g == 1:
                wait(act, low_out[k % 2], owed_low)
            if kind == "up" and g == 0 and k >= Q:
                wait(act, up_out[k % 2], owed_up)
                act.wait_ge(deg_added, k - 2)
            src = v.total[n % 4][:, 0:nj * P]
            if kind == "low":
                dst = s0[:, k, 0:nj * P] if g == 0 else s_low[k % 2][:, j0 * P - CW:(j0 + nj) * P - CW]
                act.activation(dst, src, ACT.Relu, accum_out=v.deg_low[:, k, g:g + 1]).then_inc(relued, 1)
            else:
                dst = s0[:, j0:j0 + nj, k * P:(k + 1) * P] if k < Q else s_up[k % 2][:, j0:j0 + nj, :]
                act.activation(dst, src.rearrange("p (a f) -> p a f", f=P), ACT.Relu).then_inc(relued, 1)
            if n + 1 == last_of_step[k] and k >= Q:
                act.wait_ge(relued, n + 1)
                for c0, c1 in low_stores(k):
                    end = min((k + 1) * P, c1 * CW)
                    if c1 * CW <= (k + 1) * P:
                        act.dma_start(v.s_dram[c0:c1, :, k, :].rearrange("c p n -> p c n"),
                                      s_low[k % 2][:, c0 * CW - CW:end - CW].rearrange("p (c n) -> p c n", c=c1 - c0)
                                      ).then_inc(low_out[k % 2], 16)
                    else:
                        act.dma_start(v.s_dram[c0, :, k, 0:end - c0 * CW],
                                      s_low[k % 2][:, c0 * CW - CW:end - CW]).then_inc(low_out[k % 2], 16)
                act.dma_start(v.s_dram[k // Q, :, 0:k, (k % Q) * P:(k % Q + 1) * P],
                              s_up[k % 2][:, 0:k, :]).then_inc(up_out[k % 2], 16)
            if k in APPLY_AFTER and n + 1 == last_of_step[k]:
                b = APPLY_AFTER.index(k)
                for half in range(2):
                    ln.apply(act, b, half, b)
                if b == 0:
                    act.wait_ge(ln.done, 2)
                    for half in range(2):
                        ln.high(act, 0, half, 0)
        for c in range(NC):
            act.wait_ge(d_spread, c + 1)
            act.activation(v.d_row[:, c * CW:(c + 1) * CW], v.banks[4 + c % 2][:, :], ACT.Copy).then_inc(d_row_ready, 1)

    def tensor(pe):
        pe.wait_ge(consts_made, 4 + E)
        for n, (kind, k, g, j0, nj) in enumerate(every):
            s = k % 3
            if (kind, g) == ("low", 0):
                pe.wait_ge(low_in[s], 16 * (k // 3 + 1))
                if k:
                    pe.wait_ge(up_in[s], 16 * len([kk for kk in range(1, k + 1) if kk % 3 == s]))
            if n >= LNB:
                pe.wait_ge(summed, n - LNB + 1)
            bank = v.banks[n % LNB]
            for i in range(nj):
                j = j0 + i
                src = up[s][:, j, :] if kind == "low" and j < k else low[s][:, j * P:(j + 1) * P]
                last = pe.transpose(bank[:, i * P:(i + 1) * P], src, ident[:, :])
            last.then_inc(turned, 1)
        for c in range(NC):
            pe.wait_ge(diag_ready, c + 1)
            if c >= 2:
                pe.wait_ge(d_row_ready, c - 1)
            pe.matmul(v.banks[4 + c % 2][:, :], ones[:, :],
                      v.diag_d[:, :, :].rearrange("p a f -> p (a f)"), start=True, stop=True).then_inc(d_spread, 1)

    def vector(dve):
        dve.memset(v.deg_low[:, :, :], 0.0).then_inc(deg_ready, 1)
        dve.memset(v.deg_up[:, :, :], 0.0).then_inc(deg_ready, 1)
        dve.wait_ge(deg_ready, 2)
        for n, (kind, k, g, j0, nj) in enumerate(every):
            s = k % 3
            dve.wait_ge(turned, n + 1)
            if n >= 4:
                dve.wait_ge(relued, n - 3)
            src = (low[s][:, j0 * P:(j0 + nj) * P] if kind == "low"
                   else up[s][:, j0:j0 + nj, :].rearrange("p a f -> p (a f)"))
            dve.tensor_tensor(out=v.total[n % 4][:, 0:nj * P], in0=v.banks[n % LNB][:, 0:nj * P], in1=src,
                              op=ALU.add).then_inc(summed, 1)
            if kind == "up" and j0 + nj == k:
                dve.wait_ge(relued, n + 1)
                part = s0[:, 0:k, k * P:(k + 1) * P] if k < Q else s_up[k % 2][:, 0:k, :]
                dve.tensor_reduce(out=v.deg_up[:, k, 0:k], in_=part, axis=AX.X, op=ALU.add).then_inc(deg_added, 1)
            if k in STATS_AFTER and n + 1 == last_of_step[k]:
                b = STATS_AFTER.index(k)
                for half in range(2):
                    ln.statistics(dve, b, half, b)
                for half in range(2):
                    ln.shift(dve, b, half)
        dve.wait_ge(relued, len(every))
        dve.wait_ge(deg_added, MB - 1)
        dve.tensor_reduce(out=v.deg_parts[:, 0, :], in_=v.deg_low[:, :, :], axis=AX.X, op=ALU.add)
        dve.tensor_reduce(out=v.deg_parts[:, 1, :], in_=v.deg_up[:, :, :].rearrange("p k j -> p j k"),
                          axis=AX.X, op=ALU.add).then_inc(deg_ready, 1)
        dve.wait_ge(deg_ready, 3)
        dve.tensor_tensor(out=v.deg[:, :], in0=v.deg_parts[:, 0, :], in1=v.deg_parts[:, 1, :], op=ALU.add).then_inc(deg_ready, 1)
        dve.wait_ge(deg_ready, 4)
        dve.tensor_scalar(v.deg_pos[:, :], v.deg[:, :], 0.0, None, ALU.is_gt).then_inc(deg_ready, 1)
        dve.wait_ge(deg_ready, 5)
        dve.tensor_scalar(v.deg_parts[:, 0, :], v.deg_pos[:, :], -1.0, 1.0, ALU.mult, ALU.add).then_inc(safe_step, 1)
        dve.wait_ge(safe_step, 1)
        dve.scalar_tensor_tensor(out=v.deg_safe[:, :], in0=v.deg[:, :], scalar=0.5, in1=v.deg_parts[:, 0, :],
                                 op0=ALU.mult, op1=ALU.add).then_inc(deg_ready, 1)
        dve.wait_ge(root_ready, 1)
        dve.tensor_tensor(out=v.d_inv[:, :], in0=v.deg_root[:, :], in1=v.deg_pos[:, :], op=ALU.mult).then_inc(deg_ready, 1)
        dve.wait_ge(deg_ready, 7)
        for half in range(2):
            dve.tensor_scalar(v.d_col[:, half * MB:(half + 1) * MB], v.d_inv[:, :], -0.5, None, ALU.mult).then_inc(deg_ready, 1)
        for c in range(NC):
            if c:
                dve.wait_ge(d_spread, c)
            dve.tensor_tensor(out=v.diag_d[:, :, :], in0=ident[:, None, :].to_broadcast([P, Q, P]),
                              in1=v.d_inv[:, c * Q:(c + 1) * Q][:, :, None].to_broadcast([P, Q, P]),
                              op=ALU.mult).then_inc(diag_ready, 1)

    stage = Plan()
    stage.sync, stage.gpsimd, stage.tensor, stage.scalar, stage.vector = sync, gpsimd, tensor, scalar, vector
    return stage


def wait(eng, semaphore, n):
    if not isinstance(n, int) or n > 0:
        eng.wait_ge(semaphore, n)


def graph_stage(nc, sem, v):
    B, E, MB, CW, NC, Q, U, PAIRS = v.B, v.E, v.MB, v.CW, v.NC, v.Q, v.U, v.PAIRS
    ident = v.ident
    HB = MB // 2
    acc = [v.banks[0], v.banks[1]]
    ps_w, ps_z, ps_r, ps_c = v.banks[2], v.banks[3], v.banks[4], v.banks[5]

    xn_loaded = [sem(f"xn_loaded{i}") for i in range(2)]
    half_used = sem("half_used")
    s_loaded = sem("s_loaded")
    l_scaled = sem("l_scaled")
    l_made = sem("l_made")
    l_hi_done = sem("l_hi_done")
    l_lo_done = sem("l_lo_done")
    l_lo_early = sem("l_lo_early")
    acc_copied = sem("acc_copied")
    w_done = sem("w_done")
    x_res_in = sem("x_res_in")
    x1_done = sem("x1_done")
    mv_done = sem("mv_done")
    var_done = sem("var_done")
    rstd_done = sem("rstd_done")
    z_done = sem("z_done")
    res_done = sem("res_done")
    zt_done = sem("zt_done")
    z_t_done = sem("z_t_done")
    z_hi_done = sem("z_hi_done")
    z_lo_done = sem("z_lo_done")
    logits_done = sem("logits_done")
    logits_copied = sem("logits_copied")
    idx_done = sem("idx_done")
    shift_done = sem("shift_done")
    exp_done = sem("exp_done")
    route_step = sem("route_step")
    gate_done = sem("gate_done")
    gate_turned = sem("gate_turned")
    gate_copied = sem("gate_copied")
    res_stored = sem("res_stored")
    z_stored = sem("z_stored")
    gate_stored = sem("gate_stored")
    gate_step = sem("gate_step")
    ROUTE_STEPS = 8

    ln = v.ln
    x_hi_done, x_lo_done = ln.x_hi_done, ln.x_lo_done

    def lows_before(c, r):
        return NC * c + r - 2

    def over_units(eng, body):
        for c in range(NC):
            for s in range(2):
                body(c, 0, s, B * c + s, False)
            end = PAIRS - (c in (0, NC - 1))
            with eng.Fori(1, end) as p:
                for s in range(2):
                    body(c, p, s, 2 * p + (B * c + s), False)
            if end < PAIRS:
                for s in range(2):
                    u = B * (c + 1) - 2 + s
                    body(c, PAIRS - 1, s, u, u == U - 1)

    def sync(sp):
        def load_s(c, r):
            first = (r + c) % NC * Q
            sp.wait_ge(l_lo_done, lows_before(c, r))
            sp.dma_start(v.s_st[:, :, :], v.s_dram[c][:, first:first + Q, :]).then_inc(s_loaded, 16)

        def load_x(c, b, u, half):
            wait(sp, x_lo_done, 2 * u + half - 1)
            for i in range(2):
                g = (c + 2 * half + i) % NC
                sp.dma_start(v.xn_in[half][:, i * Q:(i + 1) * Q, :],
                             v.xn_dram[b, :, g * Q:(g + 1) * Q, :]
                             ).then_inc(xn_loaded[half], 16)

        for c, b in ((c, b) for c in range(NC) for b in range(B)):
            u = B * c + b
            if u + 3 < B:
                if u == 0:
                    sp.wait_ge(l_lo_done, 2)
                    sp.wait_ge(l_lo_early, 2)
                for half in range(2):
                    ln.load(sp, u + 3, half)
            if B <= u + 1 < U:
                if u + 1 == B:
                    for half in range(2):
                        sp.wait_ge(ln.stored[half], 16 * B)
                for half in range(2):
                    load_x((u + 1) // B, (u + 1) % B, u + 1, half)
            wait(sp, x1_done, u)
            sp.dma_start(v.x_res[:, :, :],
                         v.x[b, c * CW:(c + 1) * CW, :].rearrange("(q p) f -> p q f", p=P)
                         ).then_inc(x_res_in, 16)
            if b % 2 == 0 and c + 1 < NC:
                if u == 0:
                    sp.wait_ge(l_lo_early, 2)
                    for stored, count in v.s_stores:
                        sp.wait_ge(stored, count)
                load_s(c + 1, b // 2)
            if u + 2 < B:
                for half in range(2):
                    ln.store(sp, u + 2, half)


    def tensor(pe):
        def propagate(c, s, u, half, blocks):
            for i in blocks:
                r = half * HB + i
                xh, xl = v.x_hi[2 * s + half][:, i, :], v.x_lo[2 * s + half][:, i, :]
                lh, ll = v.l_hi[c % 2][:, r, :], v.l_lo[c % 2][:, r, :]
                pe.matmul(acc[s][:, :], xh, lh, start=(r == 0), stop=False)
                pe.matmul(acc[s][:, :], xh, ll, start=False, stop=False)
                last = pe.matmul(acc[s][:, :], xl, lh, start=False, stop=(r == MB - 1))
            if blocks[-1] == HB - 1:
                last.then_inc(half_used, 1)

        def project(u):
            pe.wait_ge(acc_copied, u + 1)
            wait(pe, x1_done, u)
            for q in range(Q):
                last = pe.matmul(ps_w[:, q * P:(q + 1) * P], v.y_t[:, q * P:(q + 1) * P], v.gnn_w_sb[:, :],
                                 start=True, stop=True)
            last.then_inc(w_done, 1)

        def turn_z(u):
            pe.wait_ge(z_done, u + 1)
            for q in range(Q):
                last = pe.transpose(ps_z[:, q * P:(q + 1) * P], v.z[:, q, :], ident[:, :])
            last.then_inc(zt_done, 1)

        def route(u):
            pe.wait_ge(z_t_done, u + 1)
            wait(pe, logits_copied, u)
            for q in range(Q):
                last = pe.matmul(ps_r[:, q * E:(q + 1) * E], v.z_t[:, q * P:(q + 1) * P], v.rwt_sb[:, :],
                                 start=True, stop=True)
            last.then_inc(logits_done, 1)

        def turn_gate(u):
            pe.wait_ge(gate_done, u + 1)
            wait(pe, gate_copied, u)
            for q in range(Q):
                last = pe.transpose(ps_c[0:2 * E, q * P:(q + 1) * P], v.gate_hl[:, q, :], ident[:, :])
            last.then_inc(gate_turned, 1)

        def body(c, p, s, u, last):
            known = isinstance(u, int)
            if known and u == 0:
                pe.wait_ge(l_lo_early, 1)
                pe.wait_ge(v.small_in, 16 * v.small_loads)
            elif known and s == 0 and p == 0:
                pe.wait_ge(l_lo_done, lows_before(c + 1, 0))
            pe.wait_ge(x_lo_done, 2 * u + 1)
            wait(pe, acc_copied, u - 1)
            propagate(c, s, u, 0, range(0, Q))
            if not (known and u < 1):
                project(u - 1)
            if known and u == 0:
                pe.wait_ge(l_lo_done, 1)
            propagate(c, s, u, 0, range(Q, HB))
            if not (known and u < 2):
                turn_gate(u - 2)
            pe.wait_ge(x_lo_done, 2 * u + 2)
            if known and u == 0:
                pe.wait_ge(l_lo_early, 2)
            propagate(c, s, u, 1, range(0, Q))
            if not (known and u < 1):
                turn_z(u - 1)
            if known and u == 0:
                pe.wait_ge(l_lo_done, 2)
            propagate(c, s, u, 1, range(Q, HB))
            if not (known and u < 1):
                route(u - 1)

        over_units(pe, body)
        turn_gate(U - 2)
        project(U - 1)
        turn_z(U - 1)
        route(U - 1)
        turn_gate(U - 1)

    def scalar(act):
        def l_high(c, r):
            act.wait_ge(l_made, NC * c + r + 1)
            if c >= 2:
                act.wait_ge(half_used, 2 * B * (c - 1))
            src = v.s_st[:, :, :] if c else v.s0[:, r * Q:(r + 1) * Q, :]
            act.activation(v.l_hi[c % 2][:, bass.ds(r * Q, Q), :], src, ACT.Copy).then_inc(l_hi_done, 1)

        def x_high(u, half, s, chunk):
            if chunk:
                act.wait_ge(xn_loaded[half], 32 * u + (32 - 32 * B))
            else:
                act.wait_ge(ln.done, 2 * u + half + 1)
            wait(act, half_used, 2 * u + half - 3)
            ln.high(act, u, half, s)

        def copy_acc(u, s):
            act.wait_ge(half_used, 2 * u + 2)
            wait(act, w_done, u)
            act.activation(v.y_t[:, :], acc[s][:, :], ACT.Copy).then_inc(acc_copied, 1)

        def copy_z(u):
            act.wait_ge(zt_done, u + 1)
            wait(act, logits_done, u)
            wait(act, z_lo_done, u)
            act.activation(v.z_t[:, :], ps_z[:, :], ACT.Copy).then_inc(z_t_done, 1)
            wait(act, z_stored, 16 * u)
            act.wait_ge(z_t_done, u + 1)
            act.activation(v.z_hl[:, 0, :], v.z_t[:, :], ACT.Copy).then_inc(z_hi_done, 1)

        def copy_gate(u):
            act.wait_ge(gate_turned, u + 1)
            wait(act, gate_stored, 16 * u)
            act.activation(v.gate_t[:, :], ps_c[0:2 * E, :], ACT.Copy).then_inc(gate_copied, 1)
            act.wait_ge(gate_copied, u + 1)
            act.dma_start(v.c_dram[bass.ds(u, 1)].rearrange("a e n -> (a e) n"), v.gate_t[:, :]).then_inc(gate_stored, 16)

        def store_z(u):
            act.wait_ge(res_done, u + 1)
            act.dma_start(v.res_dram[bass.ds(u, 1)].rearrange("a p n -> (a p) n"),
                          v.res[:, :, :].rearrange("p q f -> p (q f)")).then_inc(res_stored, 16)
            act.wait_ge(z_hi_done, u + 1)
            act.wait_ge(z_lo_done, u + 1)
            act.dma_start(v.z_dram[bass.ds(u, 1)].rearrange("a p h n -> (a p) h n"),
                          v.z_hl[:, :, :].bitcast(FP32)).then_inc(z_stored, 16)

        def exps(u):
            act.wait_ge(shift_done, u + 1)
            act.activation(v.expo[:, :, :], v.shifted[:, :, :], ACT.Exp).then_inc(exp_done, 1)

        for r in range(NC):
            l_high(0, r)

        def body(c, p, s, u, last):
            known = isinstance(u, int)
            ln_ahead = c == 0 and not (known and u + 2 >= B)
            chunk = c > 0 or (known and u + 1 >= B)
            if not (known and u < 2):
                exps(u - 2)
            if not last:
                x_high(u + 1, 0, 1 - s, chunk)
                x_high(u + 1, 1, 1 - s, chunk)
            if not (known and u < 2):
                copy_gate(u - 2)
            if s == 1 and c + 1 < NC:
                l_high(c + 1, p)
            if ln_ahead:
                ln.apply(act, u + 2, 0, s)
            if not (known and u < 1):
                copy_z(u - 1)
                store_z(u - 1)
            if ln_ahead:
                ln.apply(act, u + 2, 1, s)
            copy_acc(u, s)

        over_units(act, body)
        exps(U - 2)
        copy_gate(U - 2)
        copy_z(U - 1)
        store_z(U - 1)
        exps(U - 1)
        copy_gate(U - 1)
        act.wait_ge(gate_stored, 16 * U)
        act.wait_ge(res_stored, 16 * U)
        act.wait_ge(z_stored, 16 * U)

    def gpsimd(pool):
        def l_low(c, r):
            pool.wait_ge(l_hi_done, NC * c + r + 1)
            src = v.s_st[:, :, :] if c else v.s0[:, r * Q:(r + 1) * Q, :]
            pool.tensor_tensor(out=v.l_lo[c % 2][:, bass.ds(r * Q, Q), :], in0=src,
                               in1=v.l_hi[c % 2][:, bass.ds(r * Q, Q), :].bitcast(FP32),
                               op=ALU.subtract).then_inc(l_lo_done, 1)

        def rstds(u):
            pool.wait_ge(var_done, u + 1)
            pool.tensor_tensor(out=v.rstd[:, :], in0=v.var_eps[:, :], in1=v.neg_half[:, 0:Q],
                               op=ALU.pow).then_inc(rstd_done, 1)

        l_low(0, 1)
        for stored, count in v.s_stores:
            pool.wait_ge(stored, count)
        l_low(0, 3)

        def body(c, p, s, u, last):
            known = isinstance(u, int)
            ln_ahead = c == 0 and not (known and u + 2 >= B)
            if not last:
                ln.low(pool, u + 1, 0, 1 - s)
            if ln_ahead:
                ln.root(pool, u + 2, 0)
            if not (known and u < 1):
                rstds(u - 1)
            if not last:
                ln.low(pool, u + 1, 1, 1 - s)
            if s == 1 and c + 1 < NC:
                l_low(c + 1, p)
            if ln_ahead:
                ln.root(pool, u + 2, 1)

        over_units(pool, body)
        rstds(U - 1)

    def vector(dve):
        def make_l(c, r):
            if c:
                dve.wait_ge(s_loaded, 16 * (NC * (c - 1) + r + 1))
            group = v.s_st if c else v.s0[:, r * Q:(r + 1) * Q, :]
            for j in range(Q):
                last = dve.scalar_tensor_tensor(
                    out=group[:, j, :], in0=group[:, j, :], scalar=v.d_col[:, bass.ds((r + c) * Q + j, 1)],
                    in1=v.d_row[:, c * CW:(c + 1) * CW], op0=ALU.mult, op1=ALU.mult)
            if isinstance(r, int) and r == 0:
                last.then_inc(l_scaled, 1)
                dve.wait_ge(l_scaled, c + 1)
                for j in range(Q):
                    part = group[:, j, j * P:(j + 1) * P]
                    last = dve.tensor_tensor(out=part, in0=part, in1=ident[:, :], op=ALU.add)
            last.then_inc(l_made, 1)

        def l_low_early(r):
            dve.wait_ge(l_hi_done, r + 1)
            dve.tensor_tensor(out=v.l_lo[0][:, r * Q:(r + 1) * Q, :], in0=v.s0[:, r * Q:(r + 1) * Q, :],
                              in1=v.l_hi[0][:, r * Q:(r + 1) * Q, :].bitcast(FP32), op=ALU.subtract).then_inc(l_lo_early, 1)

        def mid(u):
            dve.wait_ge(w_done, u + 1)
            dve.wait_ge(x_res_in, 16 * u + 16)
            wait(dve, res_done, u)
            dve.scalar_tensor_tensor(out=v.x1[:, :, :].rearrange("p q f -> p (q f)"), in0=ps_w[:, :], scalar=0.0,
                                     in1=v.x_res[:, :, :].rearrange("p q f -> p (q f)"),
                                     op0=ALU.max, op1=ALU.add).then_inc(x1_done, 1)
            dve.wait_ge(x1_done, u + 1)
            for q in range(Q):
                last = dve.bn_stats(out=v.stats[:, q, :], in_=v.x1[:, q, :])
            dve.drain()
            for q in range(Q):
                last = dve.bn_aggr(out=v.mv[:, q, :], in_=v.stats[:, q, :])
            last.then_inc(mv_done, 1)
            dve.wait_ge(mv_done, u + 1)
            dve.tensor_scalar(v.var_eps[:, :], v.mv[:, :, 1], v.EPS, None, ALU.add).then_inc(var_done, 1)
            dve.wait_ge(rstd_done, u + 1)
            wait(dve, zt_done, u)
            for q in range(Q):
                last = dve.tensor_scalar(v.z[:, q, :], v.x1[:, q, :], v.mv[:, q, 0:1], v.rstd[:, q:q + 1],
                                         ALU.subtract, ALU.mult)
            last.then_inc(z_done, 1)
            dve.wait_ge(z_done, u + 1)
            wait(dve, res_stored, 16 * u)
            dve.tensor_tensor(out=v.res[:, :, :], in0=v.x1[:, :, :], in1=v.z[:, :, :], op=ALU.add).then_inc(res_done, 1)

        def z_low(u):
            dve.wait_ge(z_hi_done, u + 1)
            dve.tensor_tensor(out=v.z_hl[:, 1, :], in0=v.z_t[:, :], in1=v.z_hl[:, 0, :].bitcast(FP32),
                              op=ALU.subtract).then_inc(z_lo_done, 1)

        def gates_first(u):
            dve.wait_ge(logits_done, u + 1)
            logits = v.logits
            dve.tensor_copy(logits[:, :, :].rearrange("p q e -> p (q e)"), ps_r[:, 0:Q * E]).then_inc(logits_copied, 1)
            dve.drain()
            for q in range(Q):
                dve.max(out=v.top_val[:, q, :], in_=logits[:, q, :])
            dve.drain()
            for q in range(Q):
                last = dve.max_index(out=v.top_idx[:, q, :], in_max=v.top_val[:, q, :], in_values=logits[:, q, :])
            last.then_inc(idx_done, 1)
            wait(dve, exp_done, u)
            dve.tensor_tensor(out=v.shifted[:, :, :], in0=logits[:, :, :], in1=v.top_val[:, :, 0:1].to_broadcast([P, Q, E]),
                              op=ALU.subtract).then_inc(shift_done, 1)

        def gates_second(u):
            first = ROUTE_STEPS * u
            dve.wait_ge(idx_done, u + 1)
            dve.tensor_copy(v.top_idx_f[:, :, :], v.top_idx[:, :, 0:2]).then_inc(route_step, 1)
            dve.wait_ge(route_step, first + 1)
            for n, chosen in enumerate((v.is_1st, v.is_2nd)):
                dve.tensor_tensor(out=chosen[:, :, :], in0=v.iota_e[:, :, :],
                                  in1=v.top_idx_f[:, :, n:n + 1].to_broadcast([P, Q, E]),
                                  op=ALU.is_equal).then_inc(route_step, 1)
            dve.wait_ge(route_step, first + 3)
            dve.tensor_tensor(out=v.is_top[:, :, :], in0=v.is_1st[:, :, :], in1=v.is_2nd[:, :, :],
                              op=ALU.add).then_inc(route_step, 1)
            dve.wait_ge(exp_done, u + 1)
            dve.tensor_reduce(out=v.sum_all[:, :], in_=v.expo[:, :, :], axis=AX.X, op=ALU.add)
            dve.wait_ge(route_step, first + 4)
            dve.tensor_tensor(out=v.picked[:, :, :], in0=v.expo[:, :, :], in1=v.is_top[:, :, :],
                              op=ALU.mult).then_inc(route_step, 1)
            dve.wait_ge(route_step, first + 5)
            dve.tensor_reduce(out=v.sum_top[:, :], in_=v.picked[:, :, :], axis=AX.X, op=ALU.add).then_inc(route_step, 1)
            dve.wait_ge(route_step, first + 6)
            dve.scalar_tensor_tensor(out=v.guarded[:, :], in0=v.sum_all[:, :], scalar=1e-12, in1=v.sum_top[:, :],
                                     op0=ALU.mult, op1=ALU.max).then_inc(route_step, 1)
            dve.wait_ge(route_step, first + 7)
            dve.reciprocal(v.inv_top[:, :], v.guarded[:, :]).then_inc(route_step, 1)
            dve.wait_ge(route_step, first + 8)
            dve.tensor_tensor(out=v.gate[:, :, :], in0=v.picked[:, :, :],
                              in1=v.inv_top[:, :, None].to_broadcast([P, Q, E]), op=ALU.mult).then_inc(gate_step, 1)
            dve.wait_ge(gate_step, 2 * u + 1)
            wait(dve, gate_turned, u)
            dve.tensor_copy(v.gate_hl[:, :, 0:E].bitcast(FP32R), v.gate[:, :, :]).then_inc(gate_step, 1)
            dve.wait_ge(gate_step, 2 * u + 2)
            dve.tensor_tensor(out=v.gate_hl[:, :, E:2 * E].bitcast(FP32R), in0=v.gate[:, :, :],
                              in1=v.gate_hl[:, :, 0:E], op=ALU.subtract).then_inc(gate_done, 1)

        dve.wait_ge(v.deg_ready, 9)
        dve.wait_ge(v.d_row_ready, 1)
        make_l(0, 0)
        make_l(0, 1)
        l_low_early(0)
        make_l(0, 2)
        make_l(0, 3)
        l_low_early(2)
        dve.wait_ge(v.d_row_ready, NC)

        def body(c, p, s, u, last):
            known = isinstance(u, int)
            ln_ahead = c == 0 and not (known and u + 2 >= B)
            if ln_ahead:
                ln.statistics(dve, u + 2, 0, s)
            if not (known and u < 2):
                gates_second(u - 2)
            if ln_ahead:
                ln.shift(dve, u + 2, 0)
            if not (known and u < 1):
                mid(u - 1)
            if s == 0 and c + 1 < NC:
                make_l(c + 1, p)
            if not (known and u < 1):
                z_low(u - 1)
            if ln_ahead:
                ln.statistics(dve, u + 2, 1, s)
                ln.shift(dve, u + 2, 1)
            if not (known and u < 1):
                gates_first(u - 1)

        over_units(dve, body)
        gates_second(U - 2)
        mid(U - 1)
        z_low(U - 1)
        gates_first(U - 1)
        gates_second(U - 1)

    stage = Plan()
    stage.sync, stage.gpsimd, stage.tensor, stage.scalar, stage.vector = sync, gpsimd, tensor, scalar, vector
    return stage


def build_experts(nc, sem, v):
    B, E, CW, NC, Q, U, PAIRS, R = v.B, v.E, v.CW, v.NC, v.Q, v.U, v.PAIRS, v.R
    T = E * U
    ps_h = [v.banks[0], v.banks[1]]
    ps_g = [v.banks[2], v.banks[3]]
    ps_o = [v.banks[4], v.banks[5]]
    ps_t = v.banks[6]
    LAG = 3

    consts_made = sem("e_consts_made")
    weights_in = [sem(f"weights_in{i}") for i in range(2)]
    b2_in = sem("b2_in")
    w_hi_made = sem("w_hi_made")
    w_lo_made = sem("w_lo_made")
    c_cleared = sem("c_cleared")
    z_in = [sem(f"z_in{i}") for i in range(2)]
    c_in = [sem(f"c_in{i}") for i in range(2)]
    r_in = [sem(f"r_in{i}") for i in range(2)]
    h_done = sem("h_done")
    g_done = sem("g_done")
    gelu_done = sem("gelu_done")
    gated_done = sem("gated_done")
    hi_done = sem("hi_done")
    lo_done = sem("lo_done")
    o_done = sem("o_done")
    ot_copied = sem("ot_copied")
    o_turned = sem("o_turned")
    fin_done = sem("fin_done")
    stored = [sem(f"stored{i}") for i in range(2)]

    def over_units(eng, body):
        for s in range(2):
            body(0, s, s)
        with eng.Fori(1, U // 2) as h:
            for s in range(2):
                body(h, s, 2 * h + s)

    with nc.Block() as block:

        @block.sync
        def _(sp):
            sp.dma_start(v.w_raw[:, 0, :, :], v.w1.rearrange("e d h -> d e h")).then_inc(weights_in[0], 16)
            sp.dma_start(v.w_raw[:, 1, :, :], v.w2.rearrange("e h d -> h e d")).then_inc(weights_in[1], 16)
            sp.wait_ge(consts_made, 3)
            for half in range(2):
                sp.dma_start(v.b2_raw[half * E:(half + 1) * E, :], v.b2).then_inc(b2_in, 16)
            sp.wait_ge(c_cleared, 2)

            def body(h, s, u):
                if not isinstance(u, int):
                    u = sp.snap(u)
                wait(sp, h_done, E * (u - 1) if isinstance(u, int) else E * u - E)
                sp.dma_start(v.z_e[s][:, :, :].bitcast(FP32),
                             v.z_dram[bass.ds(u, 1)].rearrange("a p h n -> (a p) h n")).then_inc(z_in[s], 16)
                wait(sp, o_done, E * (u - 1) - E + 1 if isinstance(u, int) else E * u - 2 * E + 1)
                wait(sp, g_done, E * (u - 1) if isinstance(u, int) else E * u - E)
                sp.dma_start(v.c_e[s][0:2 * E, :].bitcast(FP32),
                             v.c_dram[bass.ds(u, 1)].rearrange("a e n -> (a e) n")).then_inc(c_in[s], 16)
                wait(sp, fin_done, u - 1)
                sp.dma_start(v.r_e[s][:, :],
                             v.res_dram[bass.ds(u, 1)].rearrange("a p n -> (a p) n")).then_inc(r_in[s], 16)

            over_units(sp, body)

        @block.gpsimd
        def _(pool):
            pool.memset(v.pick_raw[:, :, :], 0.0).then_inc(consts_made, 1)
            pool.memset(v.c_zero[:, :], 0.0).then_inc(consts_made, 1)
            pool.memset(v.b2_raw[:, :], 0.0).then_inc(consts_made, 1)
            for half in range(2):
                pool.wait_ge(consts_made, 3 + half)
                pool.affine_select(out=v.pick_raw[:, :, :], in_=v.pick_raw[:, :, :], compare_op=ALU.not_equal,
                                   fill=1.0, base=-half * E, pattern=[[-1, E], [0, P]],
                                   channel_multiplier=1).then_inc(consts_made, 1)

            def store(h, s, u):
                pool.wait_ge(fin_done, u + 1)
                if isinstance(u, int):
                    b, n = u % B, u // B * CW
                else:
                    b, n = u & (B - 1), (u // B) * CW
                rows = v.out[bass.ds(b, 1)][:, bass.ds(n, CW), :]
                pool.dma_start(rows.rearrange("a (q p) f -> p (a q) f", p=P),
                               v.fin[s][:, :].rearrange("p (q f) -> p q f", f=P)).then_inc(stored[s], 16)

            over_units(pool, store)
            for s in range(2):
                pool.wait_ge(stored[s], 16 * (U // 2))

        @block.tensor
        def _(pe):
            def up_product(s, u, e):
                t = E * u + e
                k = e % 2
                if e == 0:
                    pe.wait_ge(z_in[s], 8 * u + (16 - 8 * s))
                    pe.wait_ge(c_in[s], 8 * u + (16 - 8 * s))
                wait(pe, gelu_done, t - 1)
                pe.matmul(ps_h[k][:, :], v.w1_hi[:, e, :], v.z_e[s][:, 0, :], start=True, stop=False)
                pe.matmul(ps_h[k][:, :], v.w1_hi[:, e, :], v.z_e[s][:, 1, :], start=False, stop=False)
                pe.matmul(ps_h[k][:, :], v.w1_lo[:, e, :], v.z_e[s][:, 0, :], start=False, stop=True).then_inc(h_done, 1)
                wait(pe, gated_done, t - 1)
                pe.matmul(ps_g[k][:, :], v.pick[:, e, :], v.c_e[s][:, :], start=True, stop=True).then_inc(g_done, 1)

            def down_product(s, u, e):
                t = E * u + e
                if e == 0:
                    wait(pe, ot_copied, u - 1)
                    pe.matmul(ps_o[s][:, :], v.b2_hi[:, :], v.c_e[s][:, :], start=True, stop=False)
                    pe.matmul(ps_o[s][:, :], v.b2_lo[:, :], v.c_e[s][:, :], start=False, stop=False)
                pe.wait_ge(lo_done, t + 1)
                hi, lo = v.g_hi[e % R], v.g_lo[e % R]
                pe.matmul(ps_o[s][:, :], v.w2_hi[:, e, :], hi[:, :], start=False, stop=False)
                pe.matmul(ps_o[s][:, :], v.w2_hi[:, e, :], lo[:, :], start=False, stop=False)
                pe.matmul(ps_o[s][:, :], v.w2_lo[:, e, :], hi[:, :], start=False, stop=(e == E - 1)).then_inc(o_done, 1)

            def turn_out(u):
                pe.wait_ge(ot_copied, u + 1)
                wait(pe, fin_done, u)
                for q in range(Q):
                    last = pe.transpose(ps_t[:, q * P:(q + 1) * P], v.o_t[:, q * P:(q + 1) * P], v.ident[:, :])
                last.then_inc(o_turned, 1)

            pe.wait_ge(w_hi_made, 4)
            pe.wait_ge(w_lo_made, 3)

            def body(h, s, u):
                known = isinstance(u, int)
                for e in range(E):
                    up_product(s, u, e)
                    if e >= LAG:
                        down_product(s, u, e - LAG)
                    elif not (known and u == 0):
                        down_product(1 - s, u - 1, E + e - LAG)
                    if e == 4 and not (known and u == 0):
                        turn_out(u - 1)

            over_units(pe, body)
            for e in range(E - LAG, E):
                down_product(1, U - 1, e)
            turn_out(U - 1)

        @block.scalar
        def _(act):
            for i, half in enumerate((v.w1_hi, v.w2_hi)):
                act.wait_ge(weights_in[i], 16)
                act.activation(half[:, :, :], v.w_raw[:, i, :, :], ACT.Copy).then_inc(w_hi_made, 1)
            act.wait_ge(b2_in, 32)
            act.activation(v.b2_hi[:, :], v.b2_raw[:, :], ACT.Copy).then_inc(w_hi_made, 1)
            act.wait_ge(consts_made, 5)
            act.activation(v.pick[:, :, :], v.pick_raw[:, :, :], ACT.Copy).then_inc(w_hi_made, 1)

            def gelu(u, e):
                t = E * u + e
                act.wait_ge(h_done, t + 1)
                wait(act, gated_done, t - R + 1)
                act.activation(v.act_h[e % R][:, :], ps_h[e % 2][:, :], ACT.Gelu,
                               bias=v.b1_sb[:, e:e + 1]).then_inc(gelu_done, 1)

            def high(u, e):
                t = E * u + e
                act.wait_ge(gated_done, t + 1)
                wait(act, o_done, t - R + 1)
                act.activation(v.g_hi[e % R][:, :], v.gated[e % R][:, :], ACT.Copy).then_inc(hi_done, 1)

            def copy_out(u, s):
                act.wait_ge(o_done, E * u + E)
                wait(act, o_turned, u)
                act.activation(v.o_t[:, :], ps_o[s][:, :], ACT.Copy).then_inc(ot_copied, 1)

            def body(h, s, u):
                known = isinstance(u, int)
                for e in range(E):
                    gelu(u, e)
                    if e >= 1:
                        high(u, e - 1)
                    elif not (known and u == 0):
                        high(u - 1, E - 1)
                    if e == 3 and not (known and u == 0):
                        copy_out(u - 1, 1 - s)

            over_units(act, body)
            high(U - 1, E - 1)
            copy_out(U - 1, 1)

        @block.vector
        def _(dve):
            dve.wait_ge(consts_made, 5)
            for s in range(2):
                dve.tensor_copy(v.c_e[s][:, :], v.c_zero[:, :]).then_inc(c_cleared, 1)
            for i, (hi, lo) in enumerate(((v.w1_hi, v.w1_lo), (v.w2_hi, v.w2_lo))):
                dve.wait_ge(w_hi_made, i + 1)
                dve.tensor_tensor(out=lo[:, :, :], in0=v.w_raw[:, i, :, :], in1=hi[:, :, :].bitcast(FP32),
                                  op=ALU.subtract).then_inc(w_lo_made, 1)
            dve.wait_ge(w_hi_made, 3)
            dve.tensor_tensor(out=v.b2_lo[:, :], in0=v.b2_raw[:, :], in1=v.b2_hi[:, :].bitcast(FP32),
                              op=ALU.subtract).then_inc(w_lo_made, 1)

            def scale(u, e):
                t = E * u + e
                dve.wait_ge(gelu_done, t + 1)
                dve.wait_ge(g_done, t + 1)
                wait(dve, hi_done, t - R + 1)
                dve.tensor_tensor(out=v.gated[e % R][:, :], in0=ps_g[e % 2][:, :], in1=v.act_h[e % R][:, :],
                                  op=ALU.mult).then_inc(gated_done, 1)

            def low(u, e):
                dve.wait_ge(hi_done, E * u + e + 1)
                dve.tensor_tensor(out=v.g_lo[e % R][:, :], in0=v.gated[e % R][:, :],
                                  in1=v.g_hi[e % R][:, :].bitcast(FP32), op=ALU.subtract).then_inc(lo_done, 1)

            def finish(u, s):
                dve.wait_ge(o_turned, u + 1)
                dve.wait_ge(r_in[s], 8 * u + (16 - 8 * s))
                wait(dve, stored[s], 8 * u - 8 * s)
                dve.tensor_tensor(out=v.fin[s][:, :], in0=ps_t[:, :], in1=v.r_e[s][:, :], op=ALU.add).then_inc(fin_done, 1)

            def body(h, s, u):
                known = isinstance(u, int)
                for e in range(E):
                    scale(u, e)
                    if e >= 1:
                        low(u, e - 1)
                    elif not (known and u == 0):
                        low(u - 1, E - 1)
                    if e == 6 and not (known and u == 0):
                        finish(u - 1, 1 - s)

            over_units(dve, body)
            low(U - 1, E - 1)
            finish(U - 1, 1)


_INS = ["x", "adj", "L0_gnn_W", "L0_ffn_router_w", "L0_ffn_w1", "L0_ffn_b1", "L0_ffn_w2", "L0_ffn_b2"]


def kernel(**inputs):
    import numpy as np
    import concourse.bacc as bacc
    from concourse.bass_utils import run_bass_kernel_spmd

    nc = bacc.Bacc("TRN2", target_bir_lowering=False, num_devices=1)
    arrays, args = {}, []
    for name in _INS:
        a = np.ascontiguousarray(inputs[name])
        arrays[f"in_{name}"] = a
        args.append(nc.dram_tensor(f"in_{name}", a.shape, mybir.dt.from_np(a.dtype), kind="ExternalInput").ap())
    args.append(nc.dram_tensor("out", inputs["x"].shape, FP32, kind="ExternalOutput").ap())
    gnn_moe_kernel(nc, *args)
    r = run_bass_kernel_spmd(nc, [arrays], core_ids=[0])
    return r.results[0]["out"]
```

```python
import concourse.bass as bass
from concourse import mybir
from contextlib import ExitStack

FP32 = mybir.dt.float32
FP32R = mybir.dt.float32r
U32 = mybir.dt.uint32
ALU = mybir.AluOpType
ACT = mybir.ActivationFunctionType
AX = mybir.AxisListType

P = 128


class Plan:
    pass


def gnn_moe_kernel(nc, x, adj, gnn_w, router_w, w1, b1, w2, b2, out):
    B, N, D = x.shape
    E = router_w.shape[0]
    MB = N // P
    CW = 512
    NC = N // CW
    Q = CW // P
    U = NC * B
    PAIRS = B // 2
    v = Plan()
    v.x, v.adj, v.gnn_w, v.router_w, v.w1, v.b1, v.w2, v.b2, v.out = x, adj, gnn_w, router_w, w1, b1, w2, b2, out
    v.B, v.N, v.D, v.E, v.MB, v.CW, v.NC, v.Q, v.U, v.PAIRS = B, N, D, E, MB, CW, NC, Q, U, PAIRS
    v.EPS = 1e-5
    assert D == P and N % CW == 0 and B % 2 == 0 and E == 8 and PAIRS == NC

    v.s_dram = nc.dram_tensor("s_scratch", (NC, P, MB, CW), FP32, kind="Internal").ap()
    v.xn_dram = nc.dram_tensor("xn_scratch", (B, P, MB, D), FP32, kind="Internal").ap()
    v.z_dram = nc.dram_tensor("z_scratch", (U, P, 2, CW), FP32, kind="Internal").ap()
    v.c_dram = nc.dram_tensor("c_scratch", (U, 3 * E, CW), FP32, kind="Internal").ap()
    v.res_dram = nc.dram_tensor("res_scratch", (U, P, CW), FP32, kind="Internal").ap()

    ctx = ExitStack()
    with ctx:
        limit = nc.sbuf_usable_end
        cursor = [nc.sbuf_base]

        def sb(name, shape, dt, at=None):
            c = cursor if at is None else at
            size = 4
            for n in shape[1:]:
                size *= n
            c[0] = (c[0] + 63) // 64 * 64
            t = nc.alloc_sbuf_tensor_at(name, shape, dt, offset=c[0])
            c[0] += size
            return t

        def sem(name):
            return ctx.enter_context(nc.semaphore(name))

        v.banks = [ctx.enter_context(nc.psum_tensor(f"bank{i}", [P, 512], FP32)) for i in range(8)]

        v.ident = sb("ident", [P, P], FP32)
        v.ones = sb("ones", [P, P], FP32)
        v.neg_half = sb("neg_half", [P, MB], FP32)
        v.iota_e = sb("iota_e", [P, Q, E], FP32)
        v.gnn_w_sb = sb("gnn_w_sb", [P, P], FP32)
        v.rwt_sb = sb("rwt_sb", [P, E], FP32)
        v.b1_sb = sb("b1_sb", [P, E], FP32)
        v.d_row = sb("d_row", [P, N], FP32)
        v.d_col = sb("d_col", [P, 2 * MB], FP32)
        base = cursor[0]

        at = [base]
        v.l_hi, v.l_lo, region = [None] * 2, [None] * 2, []
        for i in range(2):
            region.append(at[0])
            v.l_hi[i] = sb(f"l_hi{i}", [P, MB, CW], FP32R, at)
            region.append(at[0])
            v.l_lo[i] = sb(f"l_lo{i}", [P, MB, CW], FP32R, at)
        region.append(at[0])
        v.s_st = sb("s_st", [P, Q, CW], FP32, at)
        v.xn_in = [sb(f"xn_in{i}", [P, MB // 2, P], FP32, at) for i in range(2)]
        v.x_hi = [sb(f"x_hi{i}", [P, MB // 2, P], FP32R, at) for i in range(4)]
        v.x_lo = [sb(f"x_lo{i}", [P, MB // 2, P], FP32R, at) for i in range(4)]
        v.x_res = sb("x_res", [P, Q, P], FP32, at)
        v.y_t = sb("y_t", [P, CW], FP32, at)
        v.x1 = sb("x1", [P, Q, P], FP32, at)
        v.z = sb("z", [P, Q, P], FP32, at)
        v.res = sb("res", [P, Q, P], FP32, at)
        v.z_t = sb("z_t", [P, CW], FP32, at)
        v.z_hl = sb("z_hl", [P, 2, CW], FP32R, at)
        v.stats = sb("stats", [P, Q, 6], FP32, at)
        v.mv = sb("mv", [P, Q, 2], FP32, at)
        v.var_eps = sb("var_eps", [P, Q], FP32, at)
        v.rstd = sb("rstd", [P, Q], FP32, at)
        v.logits = sb("logits", [P, Q, E], FP32, at)
        v.top_val = sb("top_val", [P, Q, 8], FP32, at)
        v.top_idx = sb("top_idx", [P, Q, 8], U32, at)
        v.top_idx_f = sb("top_idx_f", [P, Q, 2], FP32, at)
        v.shifted = sb("shifted", [P, Q, E], FP32, at)
        v.expo = sb("expo", [P, Q, E], FP32, at)
        v.is_1st = sb("is_1st", [P, Q, E], FP32, at)
        v.is_2nd = sb("is_2nd", [P, Q, E], FP32, at)
        v.is_top = sb("is_top", [P, Q, E], FP32, at)
        v.picked = sb("picked", [P, Q, E], FP32, at)
        v.sum_all = sb("sum_all", [P, Q], FP32, at)
        v.sum_top = sb("sum_top", [P, Q], FP32, at)
        v.guarded = sb("guarded", [P, Q], FP32, at)
        v.inv_top = sb("inv_top", [P, Q], FP32, at)
        v.gate_parts = sb("gate_parts", [P, Q, 3 * E], FP32, at)
        v.gate_t = sb("gate_t", [3 * E, CW], FP32, at)
        v.x_stats = sb("x_stats", [P, MB, 6], FP32, at)
        v.x_mv = sb("x_mv", [P, MB, 2], FP32, at)
        v.x_var = sb("x_var", [P, MB], FP32, at)
        v.x_rstd = sb("x_rstd", [P, MB], FP32, at)
        v.x_shift = sb("x_shift", [P, MB], FP32, at)
        assert at[0] <= limit, at

        at = [region[0]]
        v.low = [sb(f"low{i}", [P, N], FP32, at) for i in range(3)]
        v.up = [sb(f"up{i}", [P, MB - 1, P], FP32, at) for i in range(3)]
        v.total = [sb(f"total{i}", [P, CW], FP32, at) for i in range(4)]
        assert at[0] <= region[2] - Q * CW * 4, at
        at = [region[2] - Q * CW * 4]
        v.s_low = [sb("s_low0", [P, N - CW], FP32, at), None]
        at = [region[2]]
        v.s0 = sb("s0", [P, MB, CW], FP32, at)
        v.s_low[1] = sb("s_low1", [P, N - CW], FP32, at)
        v.s_up = [sb(f"s_up{i}", [P, MB - 1, P], FP32, at) for i in range(2)]
        assert at[0] <= region[4] - Q * CW * 4, at
        v.x_raw = [sb("x_raw0", [P, MB, P], FP32, [region[4] - Q * CW * 4]),
                   sb("x_raw1", [P, MB, P], FP32, [region[3] - Q * CW * 4])]
        at = [region[4]]
        v.deg_low = sb("deg_low", [P, MB, NC], FP32, at)
        v.deg_up = sb("deg_up", [P, MB, MB], FP32, at)
        v.deg_parts = sb("deg_parts", [P, 2, MB], FP32, at)
        v.deg = sb("deg", [P, MB], FP32, at)
        v.deg_pos = sb("deg_pos", [P, MB], FP32, at)
        v.deg_safe = sb("deg_safe", [P, MB], FP32, at)
        v.deg_root = sb("deg_root", [P, MB], FP32, at)
        v.d_inv = sb("d_inv", [P, MB], FP32, at)
        v.diag_d = [sb(f"diag_d{i}", [P, Q, P], FP32, at) for i in range(3)]
        assert at[0] <= region[4] + Q * CW * 4, at

        v.w_raw = sb("w_raw", [P, 2, E, P], FP32, [region[4]])
        at = [region[0]]
        v.w1_hi = sb("w1_hi", [P, E, P], FP32R, at)
        v.w1_lo = sb("w1_lo", [P, E, P], FP32R, at)
        v.w2_hi = sb("w2_hi", [P, E, P], FP32R, at)
        v.w2_lo = sb("w2_lo", [P, E, P], FP32R, at)
        v.b2_raw = sb("b2_raw", [2 * E, P], FP32, at)
        v.b2_lo = sb("b2_lo", [E, P], FP32R, at)
        v.b2_parts = sb("b2_parts", [3 * E, P], FP32R, at)
        v.z_e = [sb(f"z_e{i}", [P, 2, CW], FP32R, at) for i in range(2)]
        v.c_parts = [sb(f"c_parts{i}", [3 * E, CW], FP32R, at) for i in range(2)]
        v.r_e = [sb(f"r_e{i}", [P, CW], FP32, at) for i in range(2)]
        v.o_t = sb("o_t", [P, CW], FP32, at)
        v.fin = [sb(f"fin{i}", [P, CW], FP32, at) for i in range(2)]
        v.c_all = [sb("c_all0", [P, E, CW], FP32, at), None]
        R = v.R = 4
        v.act_h = [sb(f"act_h{i}", [P, CW], FP32, at) for i in range(R)]
        assert at[0] <= region[2], at
        at = [region[2]]
        v.c_all[1] = sb("c_all1", [P, E, CW], FP32, at)
        v.gated = [sb(f"gated{i}", [P, CW], FP32, at) for i in range(R)]
        v.g_hi = [sb(f"g_hi{i}", [P, CW], FP32R, at) for i in range(R)]
        v.g_lo = [sb(f"g_lo{i}", [P, CW], FP32R, at) for i in range(R)]
        assert at[0] <= region[4], at

        setup, graph, experts = setup_stage(nc, sem, v), graph_stage(nc, sem, v), expert_stage(nc, sem, v)
        with nc.Block() as block:

            @block.sync
            def _(sp):
                setup.sync(sp)
                graph.sync(sp)
                experts.sync(sp)

            @block.gpsimd
            def _(pool):
                setup.gpsimd(pool)
                graph.gpsimd(pool)
                experts.gpsimd(pool)

            @block.tensor
            def _(pe):
                setup.tensor(pe)
                graph.tensor(pe)
                experts.tensor(pe)

            @block.scalar
            def _(act):
                setup.scalar(act)
                graph.scalar(act)
                experts.scalar(act)

            @block.vector
            def _(dve):
                setup.vector(dve)
                graph.vector(dve)
                experts.vector(dve)


def ln_program(nc, sem, v):
    B, MB, EPS = v.B, v.MB, v.EPS
    HB = MB // 2
    ln = Plan()
    ln.loaded = [sem(f"ln_loaded{i}") for i in range(4)]
    ln.mv_done = sem("ln_mv_done")
    ln.var_done = sem("ln_var_done")
    ln.rstd_done = sem("ln_rstd_done")
    ln.shift_done = sem("ln_shift_done")
    ln.done = sem("ln_done")
    ln.x_hi_done = sem("x_hi_done")
    ln.x_lo_done = sem("x_lo_done")
    ln.stored = [sem(f"ln_stored{i}") for i in range(2)]

    def loads_until(b, s):
        if isinstance(b, int) and b < 2:
            return 16 * (b + 1)
        return 8 * b + 32 if s == 0 else 8 * b - 8

    def statistics(dve, b, half, s):
        n = 2 * b + half
        raw = 0 if isinstance(b, int) and b < 2 else s
        ms = range(half * HB, (half + 1) * HB)
        dve.wait_ge(ln.loaded[2 * raw + half], loads_until(b, s))
        for m in ms:
            dve.bn_stats(out=v.x_stats[:, m, :], in_=v.x_raw[raw][:, m, :])
        dve.drain()
        for m in ms:
            last = dve.bn_aggr(out=v.x_mv[:, m, :], in_=v.x_stats[:, m, :])
        last.then_inc(ln.mv_done, 1)
        dve.wait_ge(ln.mv_done, n + 1)
        dve.tensor_scalar(v.x_var[:, ms[0]:ms[-1] + 1], v.x_mv[:, ms[0]:ms[-1] + 1, 1], EPS, None,
                          ALU.add).then_inc(ln.var_done, 1)

    def root(pool, b, half):
        part = slice(half * HB, (half + 1) * HB)
        wait(pool, ln.done, 2 * b + half - 1)
        pool.wait_ge(ln.var_done, 2 * b + half + 1)
        pool.tensor_tensor(out=v.x_rstd[:, part], in0=v.x_var[:, part], in1=v.neg_half[:, part],
                           op=ALU.pow).then_inc(ln.rstd_done, 1)

    def shift(dve, b, half):
        part = slice(half * HB, (half + 1) * HB)
        dve.wait_ge(ln.rstd_done, 2 * b + half + 1)
        wait(dve, ln.done, 2 * b + half - 1)
        dve.scalar_tensor_tensor(out=v.x_shift[:, part], in0=v.x_mv[:, part, 0], scalar=-1.0, in1=v.x_rstd[:, part],
                                 op0=ALU.mult, op1=ALU.mult).then_inc(ln.shift_done, 1)

    def apply(act, b, half, s):
        raw = 0 if isinstance(b, int) and b < 2 else s
        wait(act, ln.x_lo_done, 2 * b + half - 1)
        if not isinstance(b, int) or b > 0:
            act.wait_ge(ln.stored[half], 16 * b)
        act.wait_ge(ln.shift_done, 2 * b + half + 1)
        for i in range(HB):
            m = half * HB + i
            last = act.activation(v.xn_in[half][:, i, :], v.x_raw[raw][:, m, :], ACT.Identity,
                                  bias=v.x_shift[:, m:m + 1], scale=v.x_rstd[:, m:m + 1])
        last.then_inc(ln.done, 1)

    def load(sp, b, half):
        raw = 0 if b < 2 else b % 2
        if b == 1 or b == 2 or b >= 4:
            before = b - 1 if b <= 2 else b - 2
            sp.wait_ge(ln.done, 2 * before + half + 1)
        rows = v.x[b, half * HB * P:(half + 1) * HB * P, :]
        sp.dma_start(v.x_raw[raw][:, half * HB:(half + 1) * HB, :],
                     rows.rearrange("(m p) f -> p m f", p=P)).then_inc(ln.loaded[2 * raw + half], 16)

    def store(sp, b, half):
        sp.wait_ge(ln.done, 2 * b + half + 1)
        sp.dma_start(v.xn_dram[b, :, half * HB:(half + 1) * HB, :], v.xn_in[half][:, :, :]).then_inc(ln.stored[half], 16)

    def high(act, u, half, s):
        act.activation(v.x_hi[2 * s + half][:, :, :], v.xn_in[half][:, :, :], ACT.Copy).then_inc(ln.x_hi_done, 1)

    def low(pool, u, half, s):
        pool.wait_ge(ln.x_hi_done, 2 * u + half + 1)
        pool.tensor_tensor(out=v.x_lo[2 * s + half][:, :, :], in0=v.xn_in[half][:, :, :],
                           in1=v.x_hi[2 * s + half][:, :, :].bitcast(FP32), op=ALU.subtract).then_inc(ln.x_lo_done, 1)

    ln.high, ln.low = high, low
    ln.statistics, ln.root, ln.shift, ln.apply, ln.load, ln.store = statistics, root, shift, apply, load, store
    return ln


def setup_stage(nc, sem, v):
    B, N, D, E, MB, CW, NC, Q = v.B, v.N, v.D, v.E, v.MB, v.CW, v.NC, v.Q
    low, up, s_low, s_up, s0 = v.low, v.up, v.s_low, v.s_up, v.s0
    ident, ones = v.ident, v.ones
    ln = v.ln = ln_program(nc, sem, v)

    low_in = [sem(f"low_in{i}") for i in range(3)]
    up_in = [sem(f"up_in{i}") for i in range(3)]
    consts_made = v.consts_made = sem("consts_made")
    turned = sem("turned")
    summed = sem("summed")
    relued = sem("relued")
    deg_added = sem("deg_added")
    low_out = [sem(f"low_out{i}") for i in range(2)]
    up_out = [sem(f"up_out{i}") for i in range(2)]
    deg_ready = v.deg_ready = sem("deg_ready")
    safe_step = sem("safe_step")
    root_ready = sem("root_ready")
    diag_ready = sem("diag_ready")
    d_spread = sem("d_spread")
    d_row_ready = v.d_row_ready = sem("d_row_ready")
    small_in = v.small_in = sem("small_in")
    v.small_loads = 3

    def groups(k):
        out = [("low", k, g, Q * g, min(Q, k + 1 - Q * g)) for g in range(k // Q + 1)]
        out += [("up", k, g, Q * g, min(Q, k - Q * g)) for g in range((k + Q - 1) // Q)]
        return out

    every = [g for k in range(MB) for g in groups(k)]
    last_of_step = [sum(len(groups(kk)) for kk in range(k + 1)) for k in range(MB)]

    def ups_until(k):
        return sum(kind == "up" and kk <= k for kind, kk, _, _, _ in every)

    LNB = 4
    STATS_AFTER, APPLY_AFTER = (5, 9), (7, 11)

    def low_stores(k):
        whole = (k + 1) // Q
        return [(c0, c1) for c0, c1 in ((1, whole), (whole, whole + 1)) if c1 > c0 >= 1 and c0 * Q <= k]

    def stores_before(k, up_to=None):
        same = [kk for kk in range(k % 2, k, 2)]
        return 16 * sum(len(low_stores(kk)) for kk in same), 16 * sum(kk >= Q for kk in same)

    v.s_stores = [(low_out[i], stores_before(MB + i)[0]) for i in range(2)]
    v.s_stores += [(up_out[i], stores_before(MB + i)[1]) for i in range(2)]

    def sync(sp):
        for k in range(MB):
            s = k % 3
            if k >= 3:
                sp.wait_ge(summed, last_of_step[k - 3])
            sp.dma_start(low[s][:, 0:(k + 1) * P], v.adj[k * P:(k + 1) * P, 0:(k + 1) * P]).then_inc(low_in[s], 16)
            if k:
                sp.dma_start(up[s][:, 0:k, :],
                             v.adj[0:k * P, k * P:(k + 1) * P].rearrange("(j p) n -> p j n", p=P)).then_inc(up_in[s], 16)
            if k == 3:
                for half in range(2):
                    ln.load(sp, 0, half)
            if k == APPLY_AFTER[0] + 3:
                for half in range(2):
                    ln.store(sp, 0, half)
                    ln.load(sp, 1, half)
        for half in range(2):
            ln.store(sp, 1, half)
            ln.load(sp, 2, half)

    def gpsimd(pool):
        pool.memset(ident[:, :], 0.0).then_inc(consts_made, 1)
        pool.memset(ones[:, :], 1.0).then_inc(consts_made, 1)
        pool.memset(v.neg_half[:, :], -0.5).then_inc(consts_made, 1)
        for e in range(E):
            pool.memset(v.iota_e[:, :, e:e + 1], float(e)).then_inc(consts_made, 1)
        pool.wait_ge(consts_made, 3 + E)
        pool.affine_select(out=ident[:, :], in_=ident[:, :], compare_op=ALU.not_equal, fill=1.0,
                           base=0, pattern=[[-1, P]], channel_multiplier=1).then_inc(consts_made, 1)
        for b in range(2):
            for half in range(2):
                ln.root(pool, b, half)
            if b == 0:
                for half in range(2):
                    ln.low(pool, 0, half, 0)
        pool.wait_ge(deg_ready, 6)
        for part in (slice(0, Q), slice(Q, MB)):
            pool.tensor_tensor(out=v.deg_root[:, part], in0=v.deg_safe[:, part], in1=v.neg_half[:, part],
                               op=ALU.pow).then_inc(root_ready, 1)

    def scalar(act):
        act.dma_start(v.gnn_w_sb[:, :], v.gnn_w).then_inc(small_in, 16)
        with nc.allow_non_contiguous_dma(reason="small transposed constants"):
            act.dma_start(v.rwt_sb[:, :], v.router_w.rearrange("e d -> d e")).then_inc(small_in, 16)
            act.dma_start(v.b1_sb[:, :], v.b1.rearrange("e h -> h e")).then_inc(small_in, 16)
        for n, (kind, k, g, j0, nj) in enumerate(every):
            act.wait_ge(summed, n + 1)
            owed_low, owed_up = stores_before(k)
            if kind == "low" and g == 1:
                wait(act, low_out[k % 2], owed_low)
            if kind == "up" and g == 0 and k >= Q:
                wait(act, up_out[k % 2], owed_up)
                act.wait_ge(deg_added, ups_until(k - 2))
            src = v.total[n % 4][:, 0:nj * P]
            if kind == "low":
                dst = s0[:, k, 0:nj * P] if g == 0 else s_low[k % 2][:, j0 * P - CW:(j0 + nj) * P - CW]
                act.activation(dst, src, ACT.Relu, accum_out=v.deg_low[:, k, g:g + 1]).then_inc(relued, 1)
            else:
                dst = s0[:, j0:j0 + nj, k * P:(k + 1) * P] if k < Q else s_up[k % 2][:, j0:j0 + nj, :]
                act.activation(dst, src.rearrange("p (a f) -> p a f", f=P), ACT.Relu).then_inc(relued, 1)
            if n + 1 == last_of_step[k] and k >= Q:
                act.wait_ge(relued, n + 1)
                for c0, c1 in low_stores(k):
                    end = min((k + 1) * P, c1 * CW)
                    if c1 * CW <= (k + 1) * P:
                        act.dma_start(v.s_dram[c0:c1, :, k, :].rearrange("c p n -> p c n"),
                                      s_low[k % 2][:, c0 * CW - CW:end - CW].rearrange("p (c n) -> p c n", c=c1 - c0)
                                      ).then_inc(low_out[k % 2], 16)
                    else:
                        act.dma_start(v.s_dram[c0, :, k, 0:end - c0 * CW],
                                      s_low[k % 2][:, c0 * CW - CW:end - CW]).then_inc(low_out[k % 2], 16)
                act.dma_start(v.s_dram[k // Q, :, 0:k, (k % Q) * P:(k % Q + 1) * P],
                              s_up[k % 2][:, 0:k, :]).then_inc(up_out[k % 2], 16)
            if k in APPLY_AFTER and n + 1 == last_of_step[k]:
                b = APPLY_AFTER.index(k)
                for half in range(2):
                    ln.apply(act, b, half, b)
                if b == 0:
                    act.wait_ge(ln.done, 2)
                    for half in range(2):
                        ln.high(act, 0, half, 0)

        def copy_d_row(c):
            act.wait_ge(d_spread, c + 1)
            act.activation(v.d_row[:, c * CW:(c + 1) * CW], v.banks[4 + c][:, :], ACT.Copy).then_inc(d_row_ready, 1)

        v.copy_d_row = copy_d_row
        copy_d_row(0)

    def tensor(pe):
        pe.wait_ge(consts_made, 4 + E)
        for n, (kind, k, g, j0, nj) in enumerate(every):
            s = k % 3
            if (kind, g) == ("low", 0):
                pe.wait_ge(low_in[s], 16 * (k // 3 + 1))
                if k:
                    pe.wait_ge(up_in[s], 16 * len([kk for kk in range(1, k + 1) if kk % 3 == s]))
            if n >= LNB:
                pe.wait_ge(summed, n - LNB + 1)
            bank = v.banks[n % LNB]
            for i in range(nj):
                j = j0 + i
                src = up[s][:, j, :] if kind == "low" and j < k else low[s][:, j * P:(j + 1) * P]
                last = pe.transpose(bank[:, i * P:(i + 1) * P], src, ident[:, :])
            last.then_inc(turned, 1)
        for c in range(NC):
            pe.wait_ge(diag_ready, c + 1)
            pe.matmul(v.banks[4 + c][:, :], ones[:, :],
                      v.diag_d[c % 3][:, :, :].rearrange("p a f -> p (a f)"), start=True, stop=True).then_inc(d_spread, 1)

    def vector(dve):
        def make_diag(c):
            if c >= 3:
                dve.wait_ge(d_spread, c - 2)
            dve.tensor_tensor(out=v.diag_d[c % 3][:, :, :], in0=ident[:, None, :].to_broadcast([P, Q, P]),
                              in1=v.d_inv[:, c * Q:(c + 1) * Q][:, :, None].to_broadcast([P, Q, P]),
                              op=ALU.mult).then_inc(diag_ready, 1)

        v.make_diag = make_diag
        dve.memset(v.deg_low[:, :, :], 0.0).then_inc(deg_ready, 1)
        dve.memset(v.deg_up[:, :, :], 0.0).then_inc(deg_ready, 1)
        dve.wait_ge(deg_ready, 2)

        def add_rows(n):
            _, k, g, j0, nj = every[n]
            dve.wait_ge(relued, n + 1)
            part = s0[:, j0:j0 + nj, k * P:(k + 1) * P] if k < Q else s_up[k % 2][:, j0:j0 + nj, :]
            dve.tensor_reduce(out=v.deg_up[:, k, j0:j0 + nj], in_=part, axis=AX.X, op=ALU.add).then_inc(deg_added, 1)

        for n, (kind, k, g, j0, nj) in enumerate(every):
            s = k % 3
            dve.wait_ge(turned, n + 1)
            if n >= 4:
                dve.wait_ge(relued, n - 3)
            src = (low[s][:, j0 * P:(j0 + nj) * P] if kind == "low"
                   else up[s][:, j0:j0 + nj, :].rearrange("p a f -> p (a f)"))
            dve.tensor_tensor(out=v.total[n % 4][:, 0:nj * P], in0=v.banks[n % LNB][:, 0:nj * P], in1=src,
                              op=ALU.add).then_inc(summed, 1)
            if n and every[n - 1][0] == "up":
                add_rows(n - 1)
            if k in STATS_AFTER and n + 1 == last_of_step[k]:
                b = STATS_AFTER.index(k)
                for half in range(2):
                    ln.statistics(dve, b, half, b)
                for half in range(2):
                    ln.shift(dve, b, half)
        add_rows(len(every) - 1)
        dve.wait_ge(deg_added, ups_until(MB - 1))
        dve.tensor_reduce(out=v.deg_parts[:, 0, :], in_=v.deg_low[:, :, :], axis=AX.X, op=ALU.add)
        dve.tensor_reduce(out=v.deg_parts[:, 1, :], in_=v.deg_up[:, :, :].rearrange("p k j -> p j k"),
                          axis=AX.X, op=ALU.add).then_inc(deg_ready, 1)
        dve.wait_ge(deg_ready, 3)
        dve.tensor_tensor(out=v.deg[:, :], in0=v.deg_parts[:, 0, :], in1=v.deg_parts[:, 1, :], op=ALU.add).then_inc(deg_ready, 1)
        dve.wait_ge(deg_ready, 4)
        dve.tensor_scalar(v.deg_pos[:, :], v.deg[:, :], 0.0, None, ALU.is_gt).then_inc(deg_ready, 1)
        dve.wait_ge(deg_ready, 5)
        dve.tensor_scalar(v.deg_parts[:, 0, :], v.deg_pos[:, :], -1.0, 1.0, ALU.mult, ALU.add).then_inc(safe_step, 1)
        dve.wait_ge(safe_step, 1)
        dve.scalar_tensor_tensor(out=v.deg_safe[:, :], in0=v.deg[:, :], scalar=0.5, in1=v.deg_parts[:, 0, :],
                                 op0=ALU.mult, op1=ALU.add).then_inc(deg_ready, 1)
        dve.wait_ge(root_ready, 1)
        dve.tensor_tensor(out=v.d_inv[:, 0:Q], in0=v.deg_root[:, 0:Q], in1=v.deg_pos[:, 0:Q],
                          op=ALU.mult).then_inc(deg_ready, 1)
        dve.wait_ge(deg_ready, 7)
        make_diag(0)
        dve.wait_ge(root_ready, 2)
        dve.tensor_tensor(out=v.d_inv[:, Q:MB], in0=v.deg_root[:, Q:MB], in1=v.deg_pos[:, Q:MB],
                          op=ALU.mult).then_inc(deg_ready, 1)
        dve.wait_ge(deg_ready, 8)
        for half in range(2):
            dve.tensor_scalar(v.d_col[:, half * MB:(half + 1) * MB], v.d_inv[:, :], -0.5, None, ALU.mult).then_inc(deg_ready, 1)
        make_diag(1)
        make_diag(2)

    stage = Plan()
    stage.sync, stage.gpsimd, stage.tensor, stage.scalar, stage.vector = sync, gpsimd, tensor, scalar, vector
    return stage


def graph_tail(parts, e):
    for part, u in parts.get(e, []):
        part(u)


def wait(eng, semaphore, n):
    if not isinstance(n, int) or n > 0:
        eng.wait_ge(semaphore, n)


def graph_stage(nc, sem, v):
    B, E, MB, CW, NC, Q, U, PAIRS = v.B, v.E, v.MB, v.CW, v.NC, v.Q, v.U, v.PAIRS
    ident = v.ident
    HB = MB // 2
    acc = [v.banks[0], v.banks[1]]
    ps_w, ps_z, ps_r, ps_c = v.banks[2], v.banks[3], v.banks[4], v.banks[5]

    xn_loaded = [sem(f"xn_loaded{i}") for i in range(2)]
    half_used = sem("half_used")
    s_loaded = sem("s_loaded")
    l_scaled = sem("l_scaled")
    l_made = sem("l_made")
    l_hi_done = sem("l_hi_done")
    l_lo_done = sem("l_lo_done")
    l_lo_early = sem("l_lo_early")
    acc_copied = sem("acc_copied")
    w_done = sem("w_done")
    x_res_in = sem("x_res_in")
    x1_done = sem("x1_done")
    mv_done = sem("mv_done")
    var_done = sem("var_done")
    rstd_done = sem("rstd_done")
    z_done = sem("z_done")
    res_done = sem("res_done")
    zt_done = sem("zt_done")
    z_t_done = sem("z_t_done")
    z_hi_done = sem("z_hi_done")
    z_lo_done = sem("z_lo_done")
    logits_done = sem("logits_done")
    logits_copied = sem("logits_copied")
    idx_done = sem("idx_done")
    shift_done = sem("shift_done")
    exp_done = sem("exp_done")
    route_step = sem("route_step")
    gate_done = sem("gate_done")
    gate_turned = sem("gate_turned")
    gate_copied = sem("gate_copied")
    res_stored = sem("res_stored")
    z_stored = sem("z_stored")
    gate_stored = sem("gate_stored")
    gate_step = sem("gate_step")
    v.unit_stores = (z_stored, gate_stored, res_stored)
    v.half_used = half_used
    ROUTE_STEPS = 8

    ln = v.ln
    x_hi_done, x_lo_done = ln.x_hi_done, ln.x_lo_done

    def lows_before(c, r):
        return NC * c + r - 2

    def over_units(eng, body):
        for c in range(NC):
            for s in range(2):
                body(c, 0, s, B * c + s, False)
            end = PAIRS - (c in (0, NC - 1))
            with eng.Fori(1, end) as p:
                for s in range(2):
                    body(c, p, s, 2 * p + (B * c + s), False)
            if end < PAIRS:
                for s in range(2):
                    u = B * (c + 1) - 2 + s
                    body(c, PAIRS - 1, s, u, u == U - 1)

    def ln_parts(c, u):
        known = isinstance(u, int)
        return c == 0 and not (known and u + 2 >= B), c == 0 and not (known and (u == 0 or u + 1 >= B))

    def sync(sp):
        def load_s(c, r):
            first = (r + c) % NC * Q
            sp.wait_ge(l_lo_done, lows_before(c, r))
            sp.dma_start(v.s_st[:, :, :], v.s_dram[c][:, first:first + Q, :]).then_inc(s_loaded, 16)

        def load_x(c, b, u, half):
            wait(sp, x_lo_done, 2 * u + half - 1)
            for i in range(2):
                g = (c + 2 * half + i) % NC
                sp.dma_start(v.xn_in[half][:, i * Q:(i + 1) * Q, :],
                             v.xn_dram[b, :, g * Q:(g + 1) * Q, :]
                             ).then_inc(xn_loaded[half], 16)

        for c, b in ((c, b) for c in range(NC) for b in range(B)):
            u = B * c + b
            if u + 3 < B:
                if u == 0:
                    sp.wait_ge(l_lo_done, 2)
                    sp.wait_ge(l_lo_early, 2)
                for half in range(2):
                    ln.load(sp, u + 3, half)
            if B <= u + 1 < U:
                if u + 1 == B:
                    for half in range(2):
                        sp.wait_ge(ln.stored[half], 16 * B)
                for half in range(2):
                    load_x((u + 1) // B, (u + 1) % B, u + 1, half)
            wait(sp, x1_done, u)
            sp.dma_start(v.x_res[:, :, :],
                         v.x[b, c * CW:(c + 1) * CW, :].rearrange("(q p) f -> p q f", p=P)
                         ).then_inc(x_res_in, 16)
            if b % 2 == 0 and c + 1 < NC:
                if u == 0:
                    sp.wait_ge(l_lo_early, 2)
                    for stored, count in v.s_stores:
                        sp.wait_ge(stored, count)
                load_s(c + 1, b // 2)
            if 1 <= u and u + 1 < B:
                ln.store(sp, u + 1, 1)
            if u + 2 < B:
                ln.store(sp, u + 2, 0)
            if u == v.weights_unit - 1:
                sp.wait_ge(half_used, 2 * u)
                sp.wait_ge(l_lo_done, lows_before(NC, 0))
                v.load_weights(sp)
            if u == v.weights_unit + 2:
                v.place_b2_low(sp)

    def tensor(pe):
        def propagate(c, s, u, half, blocks):
            for i in blocks:
                r = half * HB + i
                xh, xl = v.x_hi[2 * s + half][:, i, :], v.x_lo[2 * s + half][:, i, :]
                lh, ll = v.l_hi[c % 2][:, r, :], v.l_lo[c % 2][:, r, :]
                pe.matmul(acc[s][:, :], xh, lh, start=(r == 0), stop=False)
                pe.matmul(acc[s][:, :], xh, ll, start=False, stop=False)
                last = pe.matmul(acc[s][:, :], xl, lh, start=False, stop=(r == MB - 1))
            if blocks[-1] == HB - 1:
                last.then_inc(half_used, 1)

        def project(u):
            pe.wait_ge(acc_copied, u + 1)
            wait(pe, x1_done, u)
            for q in range(Q):
                last = pe.matmul(ps_w[:, q * P:(q + 1) * P], v.y_t[:, q * P:(q + 1) * P], v.gnn_w_sb[:, :],
                                 start=True, stop=True)
            last.then_inc(w_done, 1)

        def turn_z(u):
            pe.wait_ge(z_done, u + 1)
            for q in range(Q):
                last = pe.transpose(ps_z[:, q * P:(q + 1) * P], v.z[:, q, :], ident[:, :])
            last.then_inc(zt_done, 1)

        def route(u):
            pe.wait_ge(z_t_done, u + 1)
            wait(pe, logits_copied, u)
            for q in range(Q):
                last = pe.matmul(ps_r[:, q * E:(q + 1) * E], v.z_t[:, q * P:(q + 1) * P], v.rwt_sb[:, :],
                                 start=True, stop=True)
            last.then_inc(logits_done, 1)

        def turn_gate(u):
            pe.wait_ge(gate_done, u + 1)
            wait(pe, gate_copied, u)
            for q in range(Q):
                last = pe.transpose(ps_c[0:3 * E, q * P:(q + 1) * P], v.gate_parts[:, q, :], ident[:, :])
            last.then_inc(gate_turned, 1)

        def body(c, p, s, u, last):
            known = isinstance(u, int)
            if known and u == 0:
                pe.wait_ge(l_lo_early, 1)
                pe.wait_ge(v.small_in, 16 * v.small_loads)
            elif known and s == 0 and p == 0:
                pe.wait_ge(l_lo_done, lows_before(c + 1, 0))
            pe.wait_ge(x_lo_done, 2 * u + 1)
            wait(pe, acc_copied, u - 1)
            propagate(c, s, u, 0, range(0, Q))
            if not (known and u < 1):
                project(u - 1)
            if known and u == 0:
                pe.wait_ge(l_lo_done, 1)
            propagate(c, s, u, 0, range(Q, HB))
            if not (known and u < 2):
                turn_gate(u - 2)
            pe.wait_ge(x_lo_done, 2 * u + 2)
            if known and u == 0:
                pe.wait_ge(l_lo_early, 2)
            propagate(c, s, u, 1, range(0, Q))
            if not (known and u < 1):
                turn_z(u - 1)
            if known and u == 0:
                pe.wait_ge(l_lo_done, 2)
            propagate(c, s, u, 1, range(Q, HB))
            if not (known and u < 1):
                route(u - 1)

        over_units(pe, body)
        project(U - 1)
        v.tail_tensor = {1: [(turn_z, U - 1), (turn_gate, U - 2)], 2: [(route, U - 1)], 7: [(turn_gate, U - 1)]}

    def scalar(act):
        def l_high(c, r):
            act.wait_ge(l_made, NC * c + r + 1)
            if c >= 2:
                act.wait_ge(half_used, 2 * B * (c - 1))
            src = v.s_st[:, :, :] if c else v.s0[:, r * Q:(r + 1) * Q, :]
            act.activation(v.l_hi[c % 2][:, bass.ds(r * Q, Q), :], src, ACT.Copy).then_inc(l_hi_done, 1)

        def x_high(u, half, s, chunk):
            if chunk:
                act.wait_ge(xn_loaded[half], 32 * u + (32 - 32 * B))
            else:
                act.wait_ge(ln.done, 2 * u + half + 1)
            wait(act, half_used, 2 * u + half - 3)
            ln.high(act, u, half, s)

        def copy_acc(u, s):
            act.wait_ge(half_used, 2 * u + 2)
            wait(act, w_done, u)
            act.activation(v.y_t[:, :], acc[s][:, :], ACT.Copy).then_inc(acc_copied, 1)

        def copy_z(u):
            act.wait_ge(zt_done, u + 1)
            wait(act, logits_done, u)
            wait(act, z_lo_done, u)
            act.activation(v.z_t[:, :], ps_z[:, :], ACT.Copy).then_inc(z_t_done, 1)
            wait(act, z_stored, 16 * u)
            act.wait_ge(z_t_done, u + 1)
            act.activation(v.z_hl[:, 0, :], v.z_t[:, :], ACT.Copy).then_inc(z_hi_done, 1)

        def copy_gate(u):
            act.wait_ge(gate_turned, u + 1)
            wait(act, gate_stored, 16 * u)
            act.activation(v.gate_t[:, :], ps_c[0:3 * E, :], ACT.Copy).then_inc(gate_copied, 1)
            act.wait_ge(gate_copied, u + 1)
            act.dma_start(v.c_dram[bass.ds(u, 1)].rearrange("a e n -> (a e) n"), v.gate_t[:, :]).then_inc(gate_stored, 16)

        def store_z(u):
            act.wait_ge(res_done, u + 1)
            act.dma_start(v.res_dram[bass.ds(u, 1)].rearrange("a p n -> (a p) n"),
                          v.res[:, :, :].rearrange("p q f -> p (q f)")).then_inc(res_stored, 16)
            act.wait_ge(z_hi_done, u + 1)
            act.wait_ge(z_lo_done, u + 1)
            act.dma_start(v.z_dram[bass.ds(u, 1)].rearrange("a p h n -> (a p) h n"),
                          v.z_hl[:, :, :].bitcast(FP32)).then_inc(z_stored, 16)

        def exps(u):
            act.wait_ge(shift_done, u + 1)
            act.activation(v.expo[:, :, :], v.shifted[:, :, :], ACT.Exp).then_inc(exp_done, 1)

        l_high(0, 0)
        v.copy_d_row(1)
        v.copy_d_row(2)
        l_high(0, 1)
        v.copy_d_row(3)
        l_high(0, 2)
        l_high(0, 3)

        def body(c, p, s, u, last):
            known = isinstance(u, int)
            ln_ahead, ln_late = ln_parts(c, u)
            chunk = c > 0 or (known and u + 1 >= B)
            if not (known and u < 2):
                exps(u - 2)
            if not last:
                x_high(u + 1, 0, 1 - s, chunk)
            if ln_late:
                ln.apply(act, u + 1, 1, 1 - s)
            if not last:
                x_high(u + 1, 1, 1 - s, chunk)
            if ln_ahead:
                ln.apply(act, u + 2, 0, s)
            if not (known and u < 2):
                copy_gate(u - 2)
            if s == 1 and c + 1 < NC:
                l_high(c + 1, p)
            if known and u == v.weights_unit:
                v.weights_high(act)
            if not (known and u < 1):
                copy_z(u - 1)
                store_z(u - 1)
            copy_acc(u, s)

        over_units(act, body)
        exps(U - 2)
        v.tail_scalar = {1: [(copy_z, U - 1), (store_z, U - 1), (copy_gate, U - 2)], 4: [(exps, U - 1)],
                         7: [(copy_gate, U - 1)]}

    def gpsimd(pool):
        def l_low(c, r):
            pool.wait_ge(l_hi_done, NC * c + r + 1)
            src = v.s_st[:, :, :] if c else v.s0[:, r * Q:(r + 1) * Q, :]
            pool.tensor_tensor(out=v.l_lo[c % 2][:, bass.ds(r * Q, Q), :], in0=src,
                               in1=v.l_hi[c % 2][:, bass.ds(r * Q, Q), :].bitcast(FP32),
                               op=ALU.subtract).then_inc(l_lo_done, 1)

        def rstds(u):
            pool.wait_ge(var_done, u + 1)
            pool.tensor_tensor(out=v.rstd[:, :], in0=v.var_eps[:, :], in1=v.neg_half[:, 0:Q],
                               op=ALU.pow).then_inc(rstd_done, 1)

        l_low(0, 1)
        for stored, count in v.s_stores:
            pool.wait_ge(stored, count)
        l_low(0, 3)

        def body(c, p, s, u, last):
            known = isinstance(u, int)
            ln_ahead, ln_late = ln_parts(c, u)
            if not last:
                ln.low(pool, u + 1, 0, 1 - s)
            if ln_ahead:
                ln.root(pool, u + 2, 0)
                ln.low(pool, u + 1, 1, 1 - s)
            if not (known and u < 1):
                rstds(u - 1)
            if not (last or ln_ahead):
                ln.low(pool, u + 1, 1, 1 - s)
            if ln_ahead:
                ln.root(pool, u + 2, 1)
            if s == 1 and c + 1 < NC:
                l_low(c + 1, p)
            if known and u == v.weights_unit:
                v.weights_low(pool)

        over_units(pool, body)
        rstds(U - 1)

    def vector(dve):
        def make_l(c, r):
            if c:
                dve.wait_ge(s_loaded, 16 * (NC * (c - 1) + r + 1))
            group = v.s_st if c else v.s0[:, r * Q:(r + 1) * Q, :]
            for j in range(Q):
                last = dve.scalar_tensor_tensor(
                    out=group[:, j, :], in0=group[:, j, :], scalar=v.d_col[:, bass.ds((r + c) * Q + j, 1)],
                    in1=v.d_row[:, c * CW:(c + 1) * CW], op0=ALU.mult, op1=ALU.mult)
            if isinstance(r, int) and r == 0:
                last.then_inc(l_scaled, 1)
                dve.wait_ge(l_scaled, c + 1)
                for j in range(Q):
                    part = group[:, j, j * P:(j + 1) * P]
                    last = dve.tensor_tensor(out=part, in0=part, in1=ident[:, :], op=ALU.add)
            last.then_inc(l_made, 1)

        def l_low_early(r):
            dve.wait_ge(l_hi_done, r + 1)
            dve.tensor_tensor(out=v.l_lo[0][:, r * Q:(r + 1) * Q, :], in0=v.s0[:, r * Q:(r + 1) * Q, :],
                              in1=v.l_hi[0][:, r * Q:(r + 1) * Q, :].bitcast(FP32), op=ALU.subtract).then_inc(l_lo_early, 1)

        def mid(u):
            dve.wait_ge(w_done, u + 1)
            dve.wait_ge(x_res_in, 16 * u + 16)
            wait(dve, res_done, u)
            dve.scalar_tensor_tensor(out=v.x1[:, :, :].rearrange("p q f -> p (q f)"), in0=ps_w[:, :], scalar=0.0,
                                     in1=v.x_res[:, :, :].rearrange("p q f -> p (q f)"),
                                     op0=ALU.max, op1=ALU.add).then_inc(x1_done, 1)
            dve.wait_ge(x1_done, u + 1)
            for q in range(Q):
                last = dve.bn_stats(out=v.stats[:, q, :], in_=v.x1[:, q, :])
            dve.drain()
            for q in range(Q):
                last = dve.bn_aggr(out=v.mv[:, q, :], in_=v.stats[:, q, :])
            last.then_inc(mv_done, 1)
            dve.wait_ge(mv_done, u + 1)
            dve.tensor_scalar(v.var_eps[:, :], v.mv[:, :, 1], v.EPS, None, ALU.add).then_inc(var_done, 1)
            dve.wait_ge(rstd_done, u + 1)
            wait(dve, zt_done, u)
            for q in range(Q):
                last = dve.tensor_scalar(v.z[:, q, :], v.x1[:, q, :], v.mv[:, q, 0:1], v.rstd[:, q:q + 1],
                                         ALU.subtract, ALU.mult)
            last.then_inc(z_done, 1)
            dve.wait_ge(z_done, u + 1)
            wait(dve, res_stored, 16 * u)
            dve.tensor_tensor(out=v.res[:, :, :], in0=v.x1[:, :, :], in1=v.z[:, :, :], op=ALU.add).then_inc(res_done, 1)

        def z_low(u):
            dve.wait_ge(z_hi_done, u + 1)
            dve.tensor_tensor(out=v.z_hl[:, 1, :], in0=v.z_t[:, :], in1=v.z_hl[:, 0, :].bitcast(FP32),
                              op=ALU.subtract).then_inc(z_lo_done, 1)

        def gates_first(u):
            dve.wait_ge(logits_done, u + 1)
            logits = v.logits
            dve.tensor_copy(logits[:, :, :].rearrange("p q e -> p (q e)"), ps_r[:, 0:Q * E]).then_inc(logits_copied, 1)
            dve.drain()
            for q in range(Q):
                dve.max(out=v.top_val[:, q, :], in_=logits[:, q, :])
            dve.drain()
            for q in range(Q):
                last = dve.max_index(out=v.top_idx[:, q, :], in_max=v.top_val[:, q, :], in_values=logits[:, q, :])
            last.then_inc(idx_done, 1)
            wait(dve, exp_done, u)
            dve.tensor_tensor(out=v.shifted[:, :, :], in0=logits[:, :, :], in1=v.top_val[:, :, 0:1].to_broadcast([P, Q, E]),
                              op=ALU.subtract).then_inc(shift_done, 1)

        def gates_second(u):
            first = ROUTE_STEPS * u
            dve.wait_ge(idx_done, u + 1)
            dve.tensor_copy(v.top_idx_f[:, :, :], v.top_idx[:, :, 0:2]).then_inc(route_step, 1)
            dve.wait_ge(route_step, first + 1)
            for n, chosen in enumerate((v.is_1st, v.is_2nd)):
                dve.tensor_tensor(out=chosen[:, :, :], in0=v.iota_e[:, :, :],
                                  in1=v.top_idx_f[:, :, n:n + 1].to_broadcast([P, Q, E]),
                                  op=ALU.is_equal).then_inc(route_step, 1)
            dve.wait_ge(route_step, first + 3)
            dve.tensor_tensor(out=v.is_top[:, :, :], in0=v.is_1st[:, :, :], in1=v.is_2nd[:, :, :],
                              op=ALU.add).then_inc(route_step, 1)
            dve.wait_ge(exp_done, u + 1)
            dve.tensor_reduce(out=v.sum_all[:, :], in_=v.expo[:, :, :], axis=AX.X, op=ALU.add)
            dve.wait_ge(route_step, first + 4)
            dve.tensor_tensor(out=v.picked[:, :, :], in0=v.expo[:, :, :], in1=v.is_top[:, :, :],
                              op=ALU.mult).then_inc(route_step, 1)
            dve.wait_ge(route_step, first + 5)
            dve.tensor_reduce(out=v.sum_top[:, :], in_=v.picked[:, :, :], axis=AX.X, op=ALU.add).then_inc(route_step, 1)
            dve.wait_ge(route_step, first + 6)
            dve.scalar_tensor_tensor(out=v.guarded[:, :], in0=v.sum_all[:, :], scalar=1e-12, in1=v.sum_top[:, :],
                                     op0=ALU.mult, op1=ALU.max).then_inc(route_step, 1)
            dve.wait_ge(route_step, first + 7)
            dve.reciprocal(v.inv_top[:, :], v.guarded[:, :]).then_inc(route_step, 1)
            dve.wait_ge(route_step, first + 8)
            gate, high, low = (v.gate_parts[:, :, i * E:(i + 1) * E] for i in range(3))
            wait(dve, gate_turned, u)
            dve.tensor_tensor(out=gate, in0=v.picked[:, :, :],
                              in1=v.inv_top[:, :, None].to_broadcast([P, Q, E]), op=ALU.mult).then_inc(gate_step, 1)
            dve.wait_ge(gate_step, 2 * u + 1)
            dve.tensor_copy(high.bitcast(FP32R), gate).then_inc(gate_step, 1)
            dve.wait_ge(gate_step, 2 * u + 2)
            dve.tensor_tensor(out=low.bitcast(FP32R), in0=gate, in1=high, op=ALU.subtract).then_inc(gate_done, 1)

        dve.wait_ge(v.deg_ready, 10)
        dve.wait_ge(v.d_row_ready, 1)
        make_l(0, 0)
        v.make_diag(3)
        make_l(0, 1)
        l_low_early(0)
        make_l(0, 2)
        make_l(0, 3)
        l_low_early(2)
        dve.wait_ge(v.d_row_ready, NC)

        def body(c, p, s, u, last):
            known = isinstance(u, int)
            ln_ahead, ln_late = ln_parts(c, u)
            if ln_late:
                ln.shift(dve, u + 1, 1)
            if ln_ahead:
                ln.statistics(dve, u + 2, 0, s)
            if not (known and u < 2):
                gates_second(u - 2)
            if ln_ahead:
                ln.shift(dve, u + 2, 0)
            if not (known and u < 1):
                mid(u - 1)
            if s == 0 and c + 1 < NC:
                make_l(c + 1, p)
            if ln_ahead:
                ln.statistics(dve, u + 2, 1, s)
            if not (known and u < 1):
                z_low(u - 1)
                gates_first(u - 1)

        over_units(dve, body)
        mid(U - 1)
        v.tail_vector = {0: [(gates_second, U - 2)], 1: [(z_low, U - 1)], 2: [(gates_first, U - 1)],
                         5: [(gates_second, U - 1)]}

    stage = Plan()
    stage.sync, stage.gpsimd, stage.tensor, stage.scalar, stage.vector = sync, gpsimd, tensor, scalar, vector
    return stage


def expert_stage(nc, sem, v):
    B, E, CW, NC, Q, U, PAIRS, R = v.B, v.E, v.CW, v.NC, v.Q, v.U, v.PAIRS, v.R
    ps_h = [v.banks[6], v.banks[7]]
    ps_o = [v.banks[0], v.banks[1]]
    ps_t = v.banks[2]
    LAG = 3
    v.weights_unit = B * (NC - 1) + 1

    weights_in = [sem(f"weights_in{i}") for i in range(2)]
    b2_in = sem("b2_in")
    b2_placed = sem("b2_placed")
    w_hi_made = sem("w_hi_made")
    w_lo_made = sem("w_lo_made")
    z_in = [sem(f"z_in{i}") for i in range(2)]
    c_in = [sem(f"c_in{i}") for i in range(2)]
    c_all_in = [sem(f"c_all_in{i}") for i in range(4)]
    r_in = [sem(f"r_in{i}") for i in range(2)]
    h_done = sem("h_done")
    gelu_done = sem("gelu_done")
    gated_done = sem("gated_done")
    hi_done = sem("hi_done")
    lo_done = sem("lo_done")
    o_done = sem("o_done")
    ot_copied = sem("ot_copied")
    o_turned = sem("o_turned")
    fin_done = sem("fin_done")
    stored = [sem(f"stored{i}") for i in range(2)]

    def load_weights(sp):
        sp.dma_start(v.w_raw[:, 0, :, :], v.w1.rearrange("e d h -> d e h")).then_inc(weights_in[0], 16)
        sp.dma_start(v.w_raw[:, 1, :, :], v.w2.rearrange("e h d -> h e d")).then_inc(weights_in[1], 16)
        for i in range(2):
            sp.dma_start(v.b2_raw[i * E:(i + 1) * E, :], v.b2).then_inc(b2_in, 16)

    def weights_high(act):
        for i, high in enumerate((v.w1_hi, v.w2_hi)):
            act.wait_ge(weights_in[i], 16)
            act.activation(high[:, :, :], v.w_raw[:, i, :, :], ACT.Copy).then_inc(w_hi_made, 1)
        act.wait_ge(b2_in, 32)
        act.activation(v.b2_parts[0:2 * E, :], v.b2_raw[:, :], ACT.Copy).then_inc(w_hi_made, 1)

    def weights_low(pool):
        for i, (high, low) in enumerate(((v.w1_hi, v.w1_lo), (v.w2_hi, v.w2_lo))):
            pool.wait_ge(w_hi_made, i + 1)
            pool.tensor_tensor(out=low[:, :, :], in0=v.w_raw[:, i, :, :], in1=high[:, :, :].bitcast(FP32),
                               op=ALU.subtract).then_inc(w_lo_made, 1)
        pool.wait_ge(w_hi_made, 3)
        pool.tensor_tensor(out=v.b2_lo[:, :], in0=v.b2_raw[0:E, :], in1=v.b2_parts[0:E, :].bitcast(FP32),
                           op=ALU.subtract).then_inc(w_lo_made, 1)

    def place_b2_low(sp):
        sp.wait_ge(w_lo_made, 3)
        sp.dma_start(v.b2_parts[2 * E:3 * E, :].bitcast(FP32), v.b2_lo[:, :].bitcast(FP32)).then_inc(b2_placed, 16)

    v.load_weights, v.weights_high, v.weights_low, v.place_b2_low = load_weights, weights_high, weights_low, place_b2_low

    def over_units(eng, body):
        for s in range(2):
            body(0, s, s)
        with eng.Fori(1, U // 2) as h:
            for s in range(2):
                body(h, s, 2 * h + s)

    def sync(sp):
        def body(h, s, u):
            known = isinstance(u, int)
            if not known:
                u = sp.snap(u)
            if known and u == 0:
                for unit_store in v.unit_stores:
                    sp.wait_ge(unit_store, 16 * 2)
            if known and u == 1:
                sp.wait_ge(v.half_used, 2 * U)
            unit_gates = v.c_dram[bass.ds(u, 1)]
            for half in range(2):
                first = half * E // 2
                wait(sp, gated_done, E * (u - 2) + first + E // 2 if not known else 0)
                sp.dma_start(v.c_all[s][:, first:first + E // 2, :],
                             unit_gates[:, first:first + E // 2, :].rearrange(
                                 "a e n -> (a e) n").partition_broadcast(P)).then_inc(c_all_in[2 * s + half], 16)
                if half == 0:
                    wait(sp, h_done, E * u - E)
                    sp.dma_start(v.z_e[s][:, :, :].bitcast(FP32),
                                 v.z_dram[bass.ds(u, 1)].rearrange("a p h n -> (a p) h n")).then_inc(z_in[s], 16)
            wait(sp, o_done, E * u - 2 * E + 1)
            for rows, part in (((0, 2 * E), (E, 3 * E)), ((2 * E, 3 * E), (E, 2 * E))):
                sp.dma_start(v.c_parts[s][rows[0]:rows[1], :].bitcast(FP32),
                             unit_gates[:, part[0]:part[1], :].rearrange("a e n -> (a e) n")).then_inc(c_in[s], 16)
            wait(sp, fin_done, u - 1)
            sp.dma_start(v.r_e[s][:, :],
                         v.res_dram[bass.ds(u, 1)].rearrange("a p n -> (a p) n")).then_inc(r_in[s], 16)
            if known and u == 1:
                for unit_store in v.unit_stores:
                    sp.wait_ge(unit_store, 16 * U)

        over_units(sp, body)

    def gpsimd(pool):
        def store(h, s, u):
            pool.wait_ge(fin_done, u + 1)
            if isinstance(u, int):
                b, n = u % B, u // B * CW
            else:
                b, n = u & (B - 1), (u // B) * CW
            rows = v.out[bass.ds(b, 1)][:, bass.ds(n, CW), :]
            pool.dma_start(rows.rearrange("a (q p) f -> p (a q) f", p=P),
                           v.fin[s][:, :].rearrange("p (q f) -> p q f", f=P)).then_inc(stored[s], 16)

        over_units(pool, store)
        for s in range(2):
            pool.wait_ge(stored[s], 16 * (U // 2))

    def tensor(pe):
        def up_product(s, u, e):
            t = E * u + e
            k = e % 2
            if e == 0:
                pe.wait_ge(z_in[s], 8 * u + (16 - 8 * s))
            wait(pe, gelu_done, t - 1)
            pe.matmul(ps_h[k][:, :], v.w1_hi[:, e, :], v.z_e[s][:, 0, :], start=True, stop=False)
            pe.matmul(ps_h[k][:, :], v.w1_hi[:, e, :], v.z_e[s][:, 1, :], start=False, stop=False)
            pe.matmul(ps_h[k][:, :], v.w1_lo[:, e, :], v.z_e[s][:, 0, :], start=False, stop=True).then_inc(h_done, 1)

        def down_product(s, u, e):
            t = E * u + e
            if e == 0:
                wait(pe, ot_copied, u - 1)
                pe.wait_ge(c_in[s], 16 * u + (32 - 16 * s))
                pe.matmul(ps_o[s][:, :], v.b2_parts[:, :], v.c_parts[s][:, :], start=True, stop=False)
            pe.wait_ge(lo_done, t + 1)
            hi, lo = v.g_hi[e % R], v.g_lo[e % R]
            pe.matmul(ps_o[s][:, :], v.w2_hi[:, e, :], hi[:, :], start=False, stop=False)
            pe.matmul(ps_o[s][:, :], v.w2_hi[:, e, :], lo[:, :], start=False, stop=False)
            pe.matmul(ps_o[s][:, :], v.w2_lo[:, e, :], hi[:, :], start=False, stop=(e == E - 1)).then_inc(o_done, 1)

        def turn_out(u):
            pe.wait_ge(ot_copied, u + 1)
            wait(pe, fin_done, u)
            for q in range(Q):
                last = pe.transpose(ps_t[:, q * P:(q + 1) * P], v.o_t[:, q * P:(q + 1) * P], v.ident[:, :])
            last.then_inc(o_turned, 1)

        pe.wait_ge(w_hi_made, 3)
        pe.wait_ge(w_lo_made, 3)
        pe.wait_ge(b2_placed, 16)

        def body(h, s, u):
            known = isinstance(u, int)
            for e in range(E):
                up_product(s, u, e)
                if e >= LAG:
                    down_product(s, u, e - LAG)
                elif not (known and u == 0):
                    down_product(1 - s, u - 1, E + e - LAG)
                if e == 4 and not (known and u == 0):
                    turn_out(u - 1)
                if known and u == 0:
                    graph_tail(v.tail_tensor, e)

        over_units(pe, body)
        for e in range(E - LAG, E):
            down_product(1, U - 1, e)
        turn_out(U - 1)

    def scalar(act):
        def gelu(u, e):
            t = E * u + e
            act.wait_ge(h_done, t + 1)
            wait(act, gated_done, t - R + 1)
            act.activation(v.act_h[e % R][:, :], ps_h[e % 2][:, :], ACT.Gelu,
                           bias=v.b1_sb[:, e:e + 1]).then_inc(gelu_done, 1)

        def high(u, e):
            t = E * u + e
            act.wait_ge(gated_done, t + 1)
            wait(act, o_done, t - R + 1)
            act.activation(v.g_hi[e % R][:, :], v.gated[e % R][:, :], ACT.Copy).then_inc(hi_done, 1)

        def copy_out(u, s):
            act.wait_ge(o_done, E * u + E)
            wait(act, o_turned, u)
            act.activation(v.o_t[:, :], ps_o[s][:, :], ACT.Copy).then_inc(ot_copied, 1)

        def body(h, s, u):
            known = isinstance(u, int)
            for e in range(E):
                gelu(u, e)
                if e >= 1:
                    high(u, e - 1)
                elif not (known and u == 0):
                    high(u - 1, E - 1)
                if e == 3 and not (known and u == 0):
                    copy_out(u - 1, 1 - s)
                if known and u == 0:
                    graph_tail(v.tail_scalar, e)

        over_units(act, body)
        high(U - 1, E - 1)
        copy_out(U - 1, 1)

    def vector(dve):
        def scale(u, s, e):
            t = E * u + e
            if e % (E // 2) == 0:
                dve.wait_ge(c_all_in[2 * s + e // (E // 2)], 8 * u + (16 - 8 * s))
            dve.wait_ge(gelu_done, t + 1)
            wait(dve, hi_done, t - R + 1)
            dve.tensor_tensor(out=v.gated[e % R][:, :], in0=v.c_all[s][:, e, :], in1=v.act_h[e % R][:, :],
                              op=ALU.mult).then_inc(gated_done, 1)

        def low(u, e):
            dve.wait_ge(hi_done, E * u + e + 1)
            dve.tensor_tensor(out=v.g_lo[e % R][:, :], in0=v.gated[e % R][:, :],
                              in1=v.g_hi[e % R][:, :].bitcast(FP32), op=ALU.subtract).then_inc(lo_done, 1)

        def finish(u, s):
            dve.wait_ge(o_turned, u + 1)
            dve.wait_ge(r_in[s], 8 * u + (16 - 8 * s))
            wait(dve, stored[s], 8 * u - 8 * s)
            dve.tensor_tensor(out=v.fin[s][:, :], in0=ps_t[:, :], in1=v.r_e[s][:, :], op=ALU.add).then_inc(fin_done, 1)

        def body(h, s, u):
            known = isinstance(u, int)
            for e in range(E):
                scale(u, s, e)
                if e >= 1:
                    low(u, e - 1)
                elif not (known and u == 0):
                    low(u - 1, E - 1)
                if e == 6 and not (known and u == 0):
                    finish(u - 1, 1 - s)
                if known and u == 0:
                    graph_tail(v.tail_vector, e)

        over_units(dve, body)
        low(U - 1, E - 1)
        finish(U - 1, 1)

    stage = Plan()
    stage.sync, stage.gpsimd, stage.tensor, stage.scalar, stage.vector = sync, gpsimd, tensor, scalar, vector
    return stage


_INS = ["x", "adj", "L0_gnn_W", "L0_ffn_router_w", "L0_ffn_w1", "L0_ffn_b1", "L0_ffn_w2", "L0_ffn_b2"]


def kernel(**inputs):
    import numpy as np
    import concourse.bacc as bacc
    from concourse.bass_utils import run_bass_kernel_spmd

    nc = bacc.Bacc("TRN2", target_bir_lowering=False, num_devices=1)
    arrays, args = {}, []
    for name in _INS:
        a = np.ascontiguousarray(inputs[name])
        arrays[f"in_{name}"] = a
        args.append(nc.dram_tensor(f"in_{name}", a.shape, mybir.dt.from_np(a.dtype), kind="ExternalInput").ap())
    args.append(nc.dram_tensor("out", inputs["x"].shape, FP32, kind="ExternalOutput").ap())
    gnn_moe_kernel(nc, *args)
    r = run_bass_kernel_spmd(nc, [arrays], core_ids=[0])
    return r.results[0]["out"]
```
